# Optimizing a Trainium2 kernel written in Bass

```python
import numpy as np
import jax
import jax.numpy as jnp

def _softmax(x, axis=-1):
    return jax.nn.softmax(x, axis=axis)

def _gelu(x):
    return jax.nn.gelu(x, approximate=True)

def _silu(x):
    return jax.nn.silu(x)

def _sigmoid(x):
    return jax.nn.sigmoid(x)

def _layernorm(x, axis=-1, eps=1e-05):
    m = jnp.mean(x, axis=axis, keepdims=True)
    v = jnp.var(x, axis=axis, keepdims=True)
    return (x - m) / jnp.sqrt(v + eps)

def _scatter_add(tgt, idx, src, axis=0):
    return tgt.at[idx].add(src)

def _segment_sum(src, seg, n):
    return jax.ops.segment_sum(src, seg, n)
kernel_name = 'mk_macaron_d1_jaxref_r8_2ec0d1'

def setup_inputs(seed: int=0):
    np.random.seed(seed)
    _w = jnp.asarray

    def _L0_attn_setup():
        import jax, jax.numpy as jnp
        import numpy as np
        B, T, D = (8, 512, 128)
        key = jax.random.key(seed)
        ks = jax.random.split(key, 7)
        s1 = 1.0 / np.sqrt(D)
        return {'x': jax.random.normal(ks[0], (B, T, D), dtype=jnp.float32), 'W1': jax.random.normal(ks[1], (D, D), dtype=jnp.float32) * s1, 'b1': jnp.zeros((D,), dtype=jnp.float32), 'w2': jax.random.normal(ks[2], (1, D), dtype=jnp.float32) * s1, 'b2': jnp.zeros((1,), dtype=jnp.float32), 'Wc': jax.random.normal(ks[3], (D, 2 * D), dtype=jnp.float32) * (1.0 / np.sqrt(2 * D)), 'bc': jnp.zeros((D,), dtype=jnp.float32)}
    _L0_attn_in = _L0_attn_setup()

    def _L0_ffn_setup():
        import jax, jax.numpy as jnp
        import numpy as np
        D_IN, D_H, D_OUT = (128, 128, 128)
        D_MOE = 512
        N_EXPERTS = 8
        TOP_K = 2
        key = jax.random.key(seed)
        ks = jax.random.split(key, 10)
        s = lambda d: 1.0 / np.sqrt(d)
        x = jax.random.normal(ks[0], (2, 256, D_IN), dtype=jnp.float32)
        W_in = jax.random.normal(ks[1], (D_IN, D_H), dtype=jnp.float32) * s(D_IN)
        b_in = jnp.zeros((D_H,), jnp.float32)
        W_gate = jax.random.normal(ks[2], (D_H, N_EXPERTS), dtype=jnp.float32) * s(D_H)
        b_gate = jnp.zeros((N_EXPERTS,), jnp.float32)
        W1 = jax.random.normal(ks[3], (N_EXPERTS, D_H, D_MOE), dtype=jnp.float32) * s(D_H)
        b1 = jnp.zeros((N_EXPERTS, D_MOE), jnp.float32)
        W2 = jax.random.normal(ks[4], (N_EXPERTS, D_MOE, D_H), dtype=jnp.float32) * s(D_MOE)
        b2 = jnp.zeros((N_EXPERTS, D_H), jnp.float32)
        W_out = jax.random.normal(ks[5], (D_H, D_OUT), dtype=jnp.float32) * s(D_H)
        b_out = jnp.zeros((D_OUT,), jnp.float32)
        return {'x': x, 'W_in': W_in, 'b_in': b_in, 'W_gate': W_gate, 'b_gate': b_gate, 'W1': W1, 'b1': b1, 'W2': W2, 'b2': b2, 'W_out': W_out, 'b_out': b_out}
    _L0_ffn_in = _L0_ffn_setup()
    _d = {'L0_attn_x': _L0_attn_in['x'], 'L0_attn_W1': _L0_attn_in['W1'], 'L0_attn_b1': _L0_attn_in['b1'], 'L0_attn_w2': _L0_attn_in['w2'], 'L0_attn_b2': _L0_attn_in['b2'], 'L0_attn_Wc': _L0_attn_in['Wc'], 'L0_attn_bc': _L0_attn_in['bc'], 'L0_ffn_W_in': _L0_ffn_in['W_in'], 'L0_ffn_b_in': _L0_ffn_in['b_in'], 'L0_ffn_W_gate': _L0_ffn_in['W_gate'], 'L0_ffn_b_gate': _L0_ffn_in['b_gate'], 'L0_ffn_W1': _L0_ffn_in['W1'], 'L0_ffn_b1': _L0_ffn_in['b1'], 'L0_ffn_W2': _L0_ffn_in['W2'], 'L0_ffn_b2': _L0_ffn_in['b2'], 'L0_ffn_W_out': _L0_ffn_in['W_out'], 'L0_ffn_b_out': _L0_ffn_in['b_out']}
    _x0 = _d['L0_attn_x']
    _d['L0_attn_x'] = jax.random.normal(jax.random.fold_in(jax.random.key(seed), 1), (4, 1024, 128), dtype=_x0.dtype)
    del _x0
    return _d

def reference(L0_attn_x, L0_attn_W1, L0_attn_b1, L0_attn_w2, L0_attn_b2, L0_attn_Wc, L0_attn_bc, L0_ffn_W_in, L0_ffn_b_in, L0_ffn_W_gate, L0_ffn_b_gate, L0_ffn_W1, L0_ffn_b1, L0_ffn_W2, L0_ffn_b2, L0_ffn_W_out, L0_ffn_b_out):

    def _L0_attn_ref(x, W1, b1, w2, b2, Wc, bc):
        import jax, jax.numpy as jnp
        import numpy as np
        B, T, D = (8, 512, 128)
        h = jnp.tanh(jnp.einsum('btd,ed->bte', x, W1) + b1)
        s = (jnp.einsum('btd,od->bto', h, w2) + b2)[..., 0]
        m = jnp.max(s, axis=1, keepdims=True)
        e = jnp.exp(s - m)
        num = jnp.cumsum(e[..., None] * x, axis=1)
        den = jnp.cumsum(e, axis=1)[..., None]
        ctx = num / den
        combined = jnp.concatenate((ctx, x), axis=2)
        out = jnp.tanh(jnp.einsum('btk,dk->btd', combined, Wc) + bc)
        return out

    def _L0_ffn_ref(x, W_in, b_in, W_gate, b_gate, W1, b1, W2, b2, W_out, b_out):
        import jax, jax.numpy as jnp
        import numpy as np
        D_IN, D_H, D_OUT = (128, 128, 128)
        D_MOE = 512
        N_EXPERTS = 8
        TOP_K = 2
        B, S, _ = x.shape
        h = x @ W_in + b_in
        t = h.reshape(B * S, -1)
        logits = t @ W_gate + b_gate
        probs = jax.nn.softmax(logits, axis=-1)
        topv, topi = jax.lax.top_k(probs, TOP_K)
        topv = topv / jnp.sum(topv, axis=-1, keepdims=True)
        route = jnp.zeros_like(probs).at[jnp.arange(t.shape[0])[:, None], topi].set(topv)
        mid = jax.nn.relu(jnp.einsum('nd,edh->neh', t, W1) + b1)
        eout = jnp.einsum('neh,ehd->ned', mid, W2) + b2
        moe_out = jnp.einsum('ne,ned->nd', route, eout)
        out = moe_out.reshape(B, S, -1) @ W_out + b_out
        return out
    x = L0_attn_x
    x = x + 0.5 * _L0_ffn_ref(_layernorm(x, axis=-1), L0_ffn_W_in, L0_ffn_b_in, L0_ffn_W_gate, L0_ffn_b_gate, L0_ffn_W1, L0_ffn_b1, L0_ffn_W2, L0_ffn_b2, L0_ffn_W_out, L0_ffn_b_out)
    x = x + _L0_attn_ref(_layernorm(x, axis=-1), L0_attn_W1, L0_attn_b1, L0_attn_w2, L0_attn_b2, L0_attn_Wc, L0_attn_bc)
    x = x + 0.5 * _L0_ffn_ref(_layernorm(x, axis=-1), L0_ffn_W_in, L0_ffn_b_in, L0_ffn_W_gate, L0_ffn_b_gate, L0_ffn_W1, L0_ffn_b1, L0_ffn_W2, L0_ffn_b2, L0_ffn_W_out, L0_ffn_b_out)
    return x

_drawn_inputs = setup_inputs


def setup_inputs(seed=0):
    import zlib

    import numpy as np

    out = dict(_drawn_inputs(seed))
    spreads = {'L0_attn_b1': (0.0, 2.0),
     'L0_attn_bc': (0.0, 0.1),
     'L0_ffn_b_in': (0.0, 0.1),
     'L0_ffn_b_gate': (0.0, 0.1),
     'L0_ffn_b1': (0.0, 0.1),
     'L0_ffn_b2': (0.0, 0.1),
     'L0_ffn_b_out': (0.0, 0.1)}
    factors = {}
    for name, (base, spread) in spreads.items():
        noise = np.random.default_rng([zlib.crc32(name.encode()), seed]).standard_normal(out[name].shape)
        drawn = base * np.exp(spread * noise) if base else spread * noise
        out[name] = jnp.asarray(drawn.astype(out[name].dtype))
    for name, factor in factors.items():
        out[name] = (out[name] * factor).astype(out[name].dtype)
    return out
```

```python
from contextlib import ExitStack

import concourse.bass as bass
from concourse import mybir


def build_program(nc, x_in, a_w1, a_b1, a_w2, a_b2, a_wc, a_bc, f_win, f_bin, f_wg, f_bg,
                  f_w1, f_b1, f_w2, f_b2, f_wout, f_bout, out):
    fp32, fp32r, bf16, i32 = (mybir.dt.float32, mybir.dt.float32r, mybir.dt.bfloat16,
                              mybir.dt.int32)
    ALU, ACT, AX = mybir.AluOpType, mybir.ActivationFunctionType, mybir.AxisListType.X
    ds = bass.ds

    P = 128
    D = f_win.shape[0]
    B, T = x_in.shape[0], x_in.shape[1]
    NE, _, DM = f_w1.shape
    NC = DM // P
    HALVES = 2
    NJ = B * T // P // HALVES
    U = 4
    NU = NJ // U
    UPB = T // P // U
    W = U * P
    TILES = 2 * NJ + NE - 1
    TRIO = 3
    STORES = TILES // TRIO
    EPS = 1e-5
    assert TILES % TRIO == 0 and D == P and NE == 8

    PLAN = [("route", 0, 0), ("route", 0, 1), ("experts", 0, 0), ("experts", 0, 1),
            ("combine", 0, 0), ("attention", 0, 0), ("route", 1, 0),
            ("combine", 0, 1), ("attention", 0, 1), ("route", 1, 1),
            ("experts", 1, 0), ("experts", 1, 1), ("combine", 1, 0), ("combine", 1, 1)]
    unit, kind_unit, middle, unit_kind, middle_kind = {}, {}, {}, [], []
    for ph in PLAN:
        if ph[0] != "experts":
            for i in range(NU):
                kind_unit[ph, i] = sum(k[0][0] == ph[0] for k in unit)
                middle[ph, i] = sum(k[0][0] != "combine" for k in unit)
                if ph[0] != "combine":
                    middle_kind.append((ph[0], kind_unit[ph, i]))
                unit[ph, i] = len(unit)
                unit_kind.append((ph[0], kind_unit[ph, i]))

    with ExitStack() as ctx:
        def sb(name, shape, dt=fp32):
            return ctx.enter_context(nc.sbuf_tensor(name, shape, dt))

        def sem(name):
            return ctx.enter_context(nc.semaphore(name))

        sorted_rows = [nc.dram_tensor(f"sorted_rows{h}", (TILES * P, D), fp32).ap() for h in range(HALVES)]
        expert_out = [nc.dram_tensor(f"expert_out{h}", (TILES * P, D), fp32).ap() for h in range(HALVES)]

        X = sb("X", [P, HALVES * NJ, D])
        H = [sb(f"H{h}", [P, NJ, D]) for h in range(HALVES)]
        w1hi, w1lo = sb("w1hi", [P, NE * DM], fp32r), sb("w1lo", [P, NE * DM], fp32r)
        w2 = sb("w2", [P, NE * NC, 2, D], fp32r)
        flat_w2 = w2[:, :, :, :].rearrange("p n a d -> p (n a d)")
        b1_all = sb("b1_all", [P, NE * DM])
        b2_pair = sb("b2_pair", [2, NE * D], fp32r)
        rows = sb("rows", [P, TILES, D])
        made = sb("made", [P, TILES, D])
        back = [sb(f"back{k}", [P, NJ, D]) for k in range(2)]
        midhi, midlo = sb("midhi", [P, TRIO, DM], fp32r), sb("midlo", [P, TRIO, DM], fp32r)
        rowThi, rowTlo = sb("rowThi", [P, TRIO, P], fp32r), sb("rowTlo", [P, TRIO, P], fp32r)
        turned_buf = sb("turned_buf", [P, 4, W])
        xT = turned_buf[:, 0:2, :]
        hT = turned_buf[:, 2:4, :]
        mid = turned_buf[:, 0:TRIO, :]
        araw = hT[:, 0, 0:3 * D].rearrange("p (a k) -> p a k", a=3)
        b2raw = H[1][0:2, 0:NE, :].rearrange("p e d -> p (e d)")
        b2hi = midhi[0:2, 0:NE * D // DM, :].rearrange("p a k -> p (a k)")
        flat_rows = rows[:, :, :].rearrange("p t d -> p (t d)")
        flat_made = made[:, :, :].rearrange("p t d -> p (t d)")
        aT = flat_rows[:, 0:NU * W]
        score = flat_rows[:, NU * W:NU * W + T]
        weight = flat_rows[:, NU * W + T:NU * W + 2 * T]
        weighted = score
        den = flat_made[:, 0:T]
        num = flat_made[:, T:T + NU * W]
        gate_out = flat_made[:, T + NU * W:T + NU * W + 2 * W].rearrange("p (s w) -> p s w", s=2)
        stage1, stage2 = flat_rows[:, 0:NE * DM], flat_made[:, 0:NE * NC * D]

        win, wout, w1T = sb("win", [P, D]), sb("wout", [P, D]), sb("w1T", [P, D])
        wcT = sb("wcT", [P, 2, D])
        w2rep, w2col = sb("w2rep", [P, P]), sb("w2col", [P, 1])
        wg = sb("wg", [P, NE])
        bin_all, bout_all, bc_all = sb("bin_all", [P, D]), sb("bout_all", [P, D]), sb("bc_all", [P, D])
        bg_all = sb("bg_all", [P, NE])
        ab1, ab2 = sb("ab1", [P, 1]), sb("ab2", [P, 1])
        row_sel, row_not = sb("row_sel", [2, 1]), sb("row_not", [2, 1])
        ident = sb("ident", [P, P])
        before, ones_bf = sb("before", [P, P], bf16), sb("ones_bf", [P, P], bf16)
        ones2f, ones2 = sb("ones2f", [2, P]), sb("ones2", [2, P], fp32r)
        one1 = sb("one1", [1, 1])
        one_col = sb("one_col", [P, 1])
        rev_i, rev = sb("rev_i", [P, NE], i32), sb("rev", [P, NE])
        step_i, step128 = sb("step_i", [P, NJ], i32), sb("step128", [P, NJ])
        tile_i, tile_no = sb("tile_i", [P, TILES], i32), sb("tile_no", [P, TILES])
        stats, mv = sb("stats", [P, NJ, 6]), sb("mv", [P, NJ, 2])
        vare, std, rstd = sb("vare", [P, NJ]), sb("std", [P, NJ]), sb("rstd", [P, NJ])
        SMALL = NJ * NE
        lg, lg2, key, hit1, hit2, ex, tmp = (
            flat_rows[:, NU * W + 2 * T + n * SMALL:NU * W + 2 * T + (n + 1) * SMALL
                      ].rearrange("p (j e) -> p j e", e=NE) for n in range(7))
        tot, cum, pos, over = (
            flat_made[:, NU * W + 2 * T + n * SMALL:NU * W + 2 * T + (n + 1) * SMALL
                      ].rearrange("p (e j) -> p e j", e=NE) for n in range(4))
        best, kbest = sb("best", [P, NJ]), sb("kbest", [P, NJ])
        ssum, rsum, p1, p2 = sb("ssum", [P, NJ]), sb("rsum", [P, NJ]), sb("p1", [P, NJ]), sb("p2", [P, NJ])
        hits = sb("hits", [P, NE, NJ], bf16)
        cnt, ctile, tend, tbase = sb("cnt", [P, NE]), sb("ctile", [P, NE]), sb("tend", [P, NE]), sb("tbase", [P, NE])
        past = sb("past", [P, TILES, NE])
        posf = sb("posf", [P, NJ])
        NQ = 2 * HALVES
        TRIOS, WIN, BITS = TILES // TRIO, TRIO + 2, 3
        owners = sb("owners", [P, TRIO * (TRIOS + 1) + 2])
        windows = sb("windows", [P, TRIOS + 1])
        windows_i = sb("windows_i", [P, NQ, TRIOS + 2], i32)
        slot = sb("slot", [P, NQ, 2, NJ], i32)
        gate = sb("gate", [P, NQ, 2, NJ])
        negmax = sb("negmax", [P, 1])
        denT, rdenT = sb("denT", [P, 8]), sb("rdenT", [P, 2, 8])

        ps = [ctx.enter_context(nc.psum_tensor(f"bank{i}", [P, 512], fp32)) for i in range(8)]

        x_in_s = [sem(f"x_loaded{c}") for c in range(4)]
        weights_s, small_s, b1_s = sem("expert_weights_loaded"), sem("small_loaded"), sem("b1_loaded")
        w2_s = sem("w2_loaded")
        consts = sem("constants_made")
        zeroed = sem("back_zeroed")
        rows_zero = sem("sorted_rows_zeroed")
        split_act, split_dve = sem("weights_hi"), sem("weights_lo")
        aw_turned, aw_copied = sem("attention_weights_turned"), sem("attention_weights_copied")
        chain = sem("vector_step")
        var_ready, std_ready = sem("variance_ready"), sem("std_ready")
        src_ready, turned, turned_out = sem("unit_source_ready"), sem("unit_turned"), sem("unit_copied")
        projected = sem("unit_projected")
        h_ready, x_added, tanh_ready = sem("experts_input_ready"), sem("x_updated"), sem("hidden_ready")
        hT_ps, hT_ready, lg_ps = sem("h_turned"), sem("hT_copied"), sem("logits_done")
        lg_read, ex_in, ex_ready = sem("logits_read"), sem("exp_input"), sem("exp_done")
        hits_ready, rank_ps, rank_read = sem("hits_ready"), sem("ranks_done"), sem("ranks_read")
        slots_ready = sem("slots_ready")
        scattered = [sem(f"scattered{h}") for h in range(HALVES)]
        rows_in = [sem(f"rows_loaded{k}") for k in range(TRIO)]
        made_out = sem("made_stored")
        row_turned, rowhi_ready, rowlo_ready = sem("tile_turned"), sem("tile_hi"), sem("tile_lo")
        up_done, mid_ready, mid_turned = sem("up_done"), sem("mid_ready"), sem("mid_turned")
        midhi_ready, midlo_ready = sem("mid_hi"), sem("mid_lo")
        down_done, made_ready = sem("down_done"), sem("tile_made")
        gathered = [sem(f"gathered{i}") for i in range(NU)]
        combined = sem("rows_combined")
        score_ps, score_ready, max_ready, weight_ready = (sem("scores_done"), sem("scores_read"),
                                                          sem("max_ready"), sem("weights_ready"))
        num_ready, out_ps, out_read = sem("sums_ready"), sem("attention_out_done"), sem("attention_out_read")
        pre_ready, gate_ready, att_x = sem("tanh_input"), sem("tanh_output"), sem("attention_added")
        den_ps, den_read = sem("denominators_turned"), sem("denominators_read")
        stored = sem("out_stored")

        block = ctx.enter_context(nc.Block())

        def q_of(ph):
            return ph[1] * HALVES + ph[2]

        def hT_used(eng, m):
            kind, a = middle_kind[m]
            eng.wait_ge(lg_ps if kind == "route" else score_ps, a + 1)

        x_rows = x_in.rearrange("b t d -> (b t) d").rearrange("(j p) d -> p j d", p=P)
        out_rows = out.rearrange("b t d -> (b t) d").rearrange("(j p) d -> p j d", p=P)

        @block.sync
        def _(sp):
            for c in range(4):
                sp.dma_start(X[:, 8 * c:8 * c + 8, :], x_rows[:, 8 * c:8 * c + 8, :]).then_inc(x_in_s[c], 16)
            sp.wait_ge(zeroed, 2)
            for h in range(HALVES):
                by_partition = sorted_rows[h].rearrange("(p r) d -> p r d", p=P)
                for k, (r0, n) in enumerate(((0, NJ), (NJ, NJ), (2 * NJ, TILES - 2 * NJ))):
                    sp.dma_start(by_partition[:, r0:r0 + n, :], back[k % 2][:, 0:n, :]).then_inc(rows_zero, 16)
            sp.dma_start(stage1.rearrange("p (e m) -> p e m", e=NE),
                         f_w1.rearrange("e d m -> d e m")).then_inc(weights_s, 16)
            sp.dma_start(stage2.rearrange("p (e c d) -> p e c d", e=NE, c=NC),
                         f_w2.rearrange("e (c p) d -> p e c d", p=P)).then_inc(w2_s, 16)
            sp.dma_start(b1_all[:, :], f_b1.rearrange("e m -> (e m)").partition_broadcast(P)).then_inc(b1_s, 16)
            for ph in PLAN:
                kind, f, h = ph
                q = q_of(ph)
                if kind == "experts":
                    sp.wait_ge(scattered[h], 16 * 2 * NJ * (f + 1))
                    if f == 0 and h == 0:
                        sp.wait_ge(split_dve, 2)
                    if f == 1 and h == 0:
                        sp.wait_ge(att_x, 2 * NU)
                        sp.wait_ge(slots_ready, 2 * HALVES)
                    base, trios = TILES * q, TILES // TRIO

                    def load(i):
                        for k in range(TRIO):
                            if q > 0 or not isinstance(i, int) or i > 0:
                                sp.wait_ge(row_turned, base + TRIO * i + k - TRIO + 1)
                            sp.dma_start(rows[:, k, :], sorted_rows[h][ds((TRIO * i + k) * P, P), :]
                                         ).then_inc(rows_in[k], 16)

                    def store(i):
                        sp.wait_ge(made_ready, base + TRIO * i + TRIO)
                        sp.dma_start(expert_out[h][ds(TRIO * i * P, TRIO * P), :].rearrange("(t p) d -> p t d", p=P),
                                     made[:, ds(TRIO * i, TRIO), :]).then_inc(made_out, 16)

                    load(0)
                    load(1)
                    with sp.Fori(2, trios) as trio:
                        load(trio)
                        store(trio - 2)
                    store(trios - 2)
                    store(trios - 1)
                if kind == "combine" and f == 1:
                    for i in range(NU):
                        sp.wait_ge(x_added, kind_unit[ph, i] + 1)
                        j = h * NJ + U * i
                        sp.dma_start(out_rows[:, j:j + U, :], X[:, j:j + U, :]).then_inc(stored, 16)
            sp.wait_ge(stored, 16 * HALVES * NU)

        @block.gpsimd
        def _(pool):
            pool.memset(back[0][:, :, :], 0.0).then_inc(zeroed, 1)
            pool.memset(back[1][:, :, :], 0.0).then_inc(zeroed, 1)
            pool.memset(ident[:, :], 0.0).then_inc(consts, 1)
            pool.memset(before[:, :], 1.0).then_inc(consts, 1)
            pool.memset(ones_bf[:, :], 1.0).then_inc(consts, 1)
            pool.memset(ones2f[:, :], 1.0).then_inc(consts, 1)
            pool.memset(one1[:, :], 1.0).then_inc(consts, 1)
            pool.memset(one_col[:, :], 1.0).then_inc(consts, 1)
            pool.memset(owners[:, :], 0.0).then_inc(consts, 1)
            pool.memset(row_sel[:, :], 0.0).then_inc(consts, 1)
            pool.memset(row_not[:, :], 1.0).then_inc(consts, 1)
            pool.wait_ge(consts, 9)
            pool.affine_select(out=ident[:, :], in_=ident[:, :], compare_op=ALU.not_equal, fill=1.0, base=0,
                               pattern=[[-1, P]], channel_multiplier=1).then_inc(consts, 1)
            pool.affine_select(out=before[:, :], in_=before[:, :], compare_op=ALU.is_gt, fill=0.0, base=0,
                               pattern=[[1, P]], channel_multiplier=-1).then_inc(consts, 1)
            pool.affine_select(out=row_sel[:, :], in_=row_sel[:, :], compare_op=ALU.not_equal, fill=1.0, base=0,
                               pattern=[[0, 1]], channel_multiplier=1).then_inc(consts, 1)
            pool.affine_select(out=row_not[:, :], in_=row_not[:, :], compare_op=ALU.not_equal, fill=0.0, base=0,
                               pattern=[[0, 1]], channel_multiplier=1).then_inc(consts, 1)
            pool.iota(rev_i[:, :], pattern=[[-1, NE]], base=NE, channel_multiplier=0).then_inc(consts, 1)
            pool.iota(step_i[:, :], pattern=[[P, NJ]], base=0, channel_multiplier=0).then_inc(consts, 1)
            pool.iota(tile_i[:, :], pattern=[[1, TILES]], base=0, channel_multiplier=0).then_inc(consts, 1)

            def scatter(f, h):
                q = f * HALVES + h
                if q == 0:
                    pool.wait_ge(rows_zero, 16 * 3 * HALVES)
                pool.wait_ge(slots_ready, q + 1)
                pool.wait_ge(h_ready, NU * (q + 1))
                if f == 1:
                    pool.wait_ge(row_turned, TILES * HALVES)
                for j in range(NJ):
                    for k in range(2):
                        pool.indirect_dma_start(
                            sorted_rows[h], bass.IndirectOffsetOnAxis(slot[:, q, k, j:j + 1], 0),
                            H[h][:, j, :], None).then_inc(scattered[h], 16)

            def gather(f, h):
                q = f * HALVES + h
                pool.wait_ge(made_out, 16 * STORES * (q + 1))
                for i in range(NU):
                    if q > 0:
                        last = ("combine", (q - 1) // HALVES, (q - 1) % HALVES)
                        pool.wait_ge(turned, unit[last, i] + 1)
                    for j in range(U * i, U * i + U):
                        for k in range(2):
                            pool.indirect_dma_start(
                                back[k][:, j, :], None, expert_out[h],
                                bass.IndirectOffsetOnAxis(slot[:, q, k, j:j + 1], 0)).then_inc(gathered[i], 16)

            for f in range(2):
                scatter(f, 0)
                scatter(f, 1)
                gather(f, 0)
                gather(f, 1)

        @block.scalar
        def _(act):
            for dst, src in ((win, f_win), (wout, f_wout), (wg, f_wg),
                             (bin_all, f_bin.partition_broadcast(P)), (bg_all, f_bg.partition_broadcast(P)),
                             (bout_all, f_bout.partition_broadcast(P)), (bc_all, a_bc.partition_broadcast(P)),
                             (ab1, a_b1.rearrange("(p a) -> p a", a=1)),
                             (ab2, a_b2.partition_broadcast(P)),
                             (w2col, a_w2.rearrange("a p -> p a")),
                             (b2raw, f_b2.rearrange("e d -> (e d)").partition_broadcast(2))):
                act.dma_start(dst[:, :], src).then_inc(small_s, 16)
            act.dma_start(araw[:, 0, :], a_w1).then_inc(small_s, 16)
            act.dma_start(araw[:, 1:3, :], a_wc.rearrange("p (a k) -> p a k", a=2)).then_inc(small_s, 16)

            def copy_unit(ph, i, dst):
                act.wait_ge(turned, unit[ph, i] + 1)
                act.activation(dst, ps[unit[ph, i] % 2][:, :], ACT.Copy).then_inc(turned_out, 1)

            def xT_of(ph, i):
                n = unit[ph, i]
                if n >= 2:
                    act.wait_ge(projected, n - 1)
                copy_unit(ph, i, xT[:, n % 2, :])

            def root(n):
                act.wait_ge(var_ready, n + 1)
                act.activation(std[:, :], vare[:, :], ACT.Sqrt).then_inc(std_ready, 1)

            act.wait_ge(aw_turned, 1)
            act.activation(w1T[:, :], ps[7][:, 0:D], ACT.Copy).then_inc(aw_copied, 1)
            act.activation(wcT[:, :, :], ps[7][:, D:3 * D], ACT.Copy).then_inc(aw_copied, 1)
            lns = 0
            for ph in PLAN:
                kind, f, h = ph
                q = q_of(ph)
                if kind == "route":
                    root(lns)
                    lns += 1
                    for i in range(NU + 2):
                        if i < NU:
                            xT_of(ph, i)
                        if i >= 2:
                            m = middle[ph, i - 2]
                            act.wait_ge(hT_ps, kind_unit[ph, i - 2] + 1)
                            if m >= 2:
                                hT_used(act, m - 2)
                            act.activation(hT[:, m % 2, :], ps[4 + m % 2][:, :], ACT.Copy).then_inc(hT_ready, 1)
                    act.wait_ge(ex_in, q + 1)
                    act.activation(ex[:, :, :], tmp[:, :, :], ACT.Exp).then_inc(ex_ready, 1)
                    if q == 0:
                        act.wait_ge(weights_s, 16)
                        act.activation(w1hi[:, :], stage1, ACT.Copy).then_inc(split_act, 1)
                        act.wait_ge(w2_s, 16)
                        act.activation(w2[:, :, 0, :], stage2.rearrange("p (n d) -> p n d", d=D), ACT.Copy).then_inc(split_act, 1)
                elif kind == "combine":
                    for i in range(NU):
                        xT_of(ph, i)
                elif kind == "attention":
                    root(lns)
                    lns += 1
                    def hidden(i):
                        n, m, a = unit[ph, i], middle[ph, i], kind_unit[ph, i]
                        act.wait_ge(projected, n + 1)
                        if m >= 2:
                            hT_used(act, m - 2)
                        act.activation(hT[:, m % 2, :], ps[2 + n % 2][:, :], ACT.Tanh,
                                       bias=ab1[:, :]).then_inc(tanh_ready, 1)

                    def scores(i):
                        m, a = middle[ph, i], kind_unit[ph, i]
                        act.wait_ge(score_ps, a + 1)
                        if i % UPB == 0 and a >= UPB:
                            act.wait_ge(num_ready, a // UPB)
                        act.activation(score[:, (i % UPB) * W:(i % UPB + 1) * W], ps[4 + m % 2][:, :],
                                       ACT.Identity, bias=ab2[:, :]).then_inc(score_ready, 1)

                    def exps(b):
                        n = h * (NU // UPB) + b
                        act.wait_ge(max_ready, n + 1)
                        act.wait_ge(score_ready, UPB * (n + 1))
                        if n >= 1:
                            act.wait_ge(num_ready, n)
                        act.activation(weight, score, ACT.Exp, bias=negmax[:, :]).then_inc(weight_ready, 1)

                    def outs(i):
                        a = kind_unit[ph, i]
                        act.wait_ge(pre_ready, a + 1)
                        act.activation(gate_out[:, a % 2, :], gate_out[:, a % 2, :], ACT.Tanh).then_inc(gate_ready, 1)

                    for i in range(NU + 2):
                        if i < NU:
                            copy_unit(ph, i, aT[:, i * W:(i + 1) * W])
                        if 1 <= i <= NU:
                            hidden(i - 1)
                        if i >= 2:
                            scores(i - 2)
                            if (i - 1) % UPB == 0:
                                exps((i - 1) // UPB - 1)
                    for i in range(NU):
                        outs(i)
                else:
                    base = TILES * q

                    def row_hi(s, k):
                        act.wait_ge(row_turned, base + s + 1)
                        act.activation(rowThi[:, k, :], ps[6][:, 0:P], ACT.Copy).then_inc(rowhi_ready, 1)

                    def mid_hi(s, k):
                        act.wait_ge(mid_turned, base + s + 1)
                        act.activation(midhi[:, k, :], ps[3 + k][:, :], ACT.Relu).then_inc(midhi_ready, 1)

                    def turn(s, k):
                        row_hi(s + 1, (k + 1) % TRIO)
                        mid_hi(s - 1, (k + 2) % TRIO)

                    row_hi(0, 0)
                    row_hi(1, 1)
                    row_hi(2, 2)
                    mid_hi(0, 0)
                    turn(2, 2)
                    with act.Fori(1, TILES // TRIO - 1) as trio:
                        for k in range(TRIO):
                            turn(trio * TRIO + k, k)
                    turn(TILES - 3, 0)
                    turn(TILES - 2, 1)
                    mid_hi(TILES - 2, 1)
                    mid_hi(TILES - 1, 2)

        @block.vector
        def _(dve):
            steps = [0]

            def did(ins):
                steps[0] += 1
                return ins.then_inc(chain, 1)

            def settle():
                dve.wait_ge(chain, steps[0])

            def over_e(ap):
                return ap.unsqueeze(2).to_broadcast([P, NJ, NE])

            def over_j(ap):
                return ap.unsqueeze(2).to_broadcast([P, NE, NJ])

            def over_blocks(ap, n):
                return ap.unsqueeze(1).to_broadcast([P, n, D])

            def blocks(ap):
                return ap.rearrange("p (u d) -> p u d", u=U)

            dve_window = dve.alloc_register("vector_window")
            dve.wait_ge(consts, 16)
            did(dve.tensor_copy(rev[:, :], rev_i[:, :]))
            did(dve.tensor_copy(step128[:, :], step_i[:, :]))
            did(dve.tensor_copy(tile_no[:, :], tile_i[:, :]))
            did(dve.tensor_copy(ones2[:, :], ones2f[:, :]))
            dve.wait_ge(small_s, 16 * 13)
            did(dve.tensor_scalar(bout_all[:, :], bout_all[:, :], 0.5, None, ALU.mult))
            did(dve.tensor_copy(w2rep[:, :], w2col[:, 0:1].to_broadcast([P, P])))
            did(dve.tensor_copy(b2hi[:, :], b2raw[:, :]))
            settle()
            did(dve.tensor_tensor(b2raw[:, :], b2raw[:, :], b2hi[:, :].bitcast(fp32), ALU.subtract))
            settle()
            did(dve.tensor_scalar(b2raw[:, :], b2raw[:, :], row_not[:, :], None, ALU.mult))
            settle()
            did(dve.scalar_tensor_tensor(b2_pair[:, :], b2hi[:, :].bitcast(fp32), row_sel[:, :], b2raw[:, :],
                                         ALU.mult, ALU.add))
            settle()

            def layernorm(ph):
                kind, f, h = ph
                j0 = h * NJ
                n = layernorm.count
                layernorm.count += 1
                if kind == "route" and f == 0:
                    for c in (2 * h, 2 * h + 1):
                        dve.wait_ge(x_in_s[c], 16)
                elif kind == "attention":
                    dve.wait_ge(x_added, NU * (h + 1))
                else:
                    dve.wait_ge(att_x, NU * (h + 1))
                for j in range(NJ):
                    did(dve.bn_stats(stats[:, j, :], X[:, j0 + j, :]))
                settle()
                for j in range(NJ):
                    did(dve.bn_aggr(mv[:, j, :], stats[:, j, :]))
                settle()
                dve.tensor_scalar(vare[:, :], mv[:, :, 1], EPS, None, ALU.add).then_inc(var_ready, 1)
                dve.wait_ge(std_ready, n + 1)
                did(dve.reciprocal(rstd[:, :], std[:, :]))
                settle()
                if kind == "attention":
                    dve.wait_ge(scattered[h], 16 * 2 * NJ)
                if kind == "route" and f == 1:
                    att = ("attention", 0, h)
                    dve.wait_ge(turned, unit[att, NU - 1] + 1)
                for i in range(NU):
                    for j in range(U * i, U * i + U):
                        last = dve.tensor_scalar(H[h][:, j, :], X[:, j0 + j, :], mv[:, j, 0:1],
                                                 rstd[:, j:j + 1], ALU.subtract, ALU.mult)
                    last.then_inc(src_ready, 1)

            layernorm.count = 0

            def first_hit(values, hit):
                did(dve.tensor_reduce(best[:, :], values[:, :, :], AX, ALU.max))
                settle()
                did(dve.tensor_tensor(hit[:, :, :], values[:, :, :], over_e(best[:, :]), ALU.is_equal))
                settle()
                did(dve.tensor_tensor(key[:, :, :], hit[:, :, :], rev[:, :].unsqueeze(1).to_broadcast([P, NJ, NE]),
                                      ALU.mult))
                settle()
                did(dve.tensor_reduce(kbest[:, :], key[:, :, :], AX, ALU.max))
                settle()
                did(dve.tensor_tensor(hit[:, :, :], key[:, :, :], over_e(kbest[:, :]), ALU.is_equal))

            for ph in PLAN:
                kind, f, h = ph
                q = q_of(ph)
                if kind == "route":
                    layernorm(ph)
                    for i in range(NU):
                        n = unit[ph, i]
                        dve.wait_ge(projected, n + 1)
                        dve.tensor_tensor(H[h][:, U * i:U * i + U, :], blocks(ps[2 + n % 2][:, :]),
                                          over_blocks(bin_all[:, :], U), ALU.add).then_inc(h_ready, 1)
                    dve.wait_ge(lg_ps, NU * (q + 1))
                    dve.tensor_tensor(lg[:, :, :], ps[6][:, 0:NJ * NE].rearrange("p (j e) -> p j e", e=NE),
                                      bg_all[:, :].unsqueeze(1).to_broadcast([P, NJ, NE]), ALU.add
                                      ).then_inc(lg_read, 1)
                    dve.wait_ge(lg_read, q + 1)
                    first_hit(lg, hit1)
                    settle()
                    dve.tensor_tensor(tmp[:, :, :], lg[:, :, :], over_e(best[:, :]), ALU.subtract).then_inc(ex_in, 1)
                    did(dve.scalar_tensor_tensor(lg2[:, :, :], hit1[:, :, :], -3.0e38, lg[:, :, :],
                                                 ALU.mult, ALU.add))
                    settle()
                    dve.wait_ge(ex_in, q + 1)
                    first_hit(lg2, hit2)
                    settle()
                    dve.tensor_tensor(hits[:, :, :].rearrange("p e j -> p j e"), hit1[:, :, :], hit2[:, :, :],
                                      ALU.add).then_inc(hits_ready, 1)
                    dve.wait_ge(ex_ready, q + 1)
                    did(dve.tensor_reduce(ssum[:, :], ex[:, :, :], AX, ALU.add))
                    did(dve.tensor_tensor(tmp[:, :, :], ex[:, :, :], hit1[:, :, :], ALU.mult))
                    did(dve.tensor_tensor(key[:, :, :], ex[:, :, :], hit2[:, :, :], ALU.mult))
                    settle()
                    did(dve.reciprocal(rsum[:, :], ssum[:, :]))
                    did(dve.tensor_reduce(p1[:, :], tmp[:, :, :], AX, ALU.add))
                    did(dve.tensor_reduce(p2[:, :], key[:, :, :], AX, ALU.add))
                    settle()
                    did(dve.tensor_tensor(p1[:, :], p1[:, :], rsum[:, :], ALU.mult))
                    did(dve.tensor_tensor(p2[:, :], p2[:, :], rsum[:, :], ALU.mult))
                    settle()
                    did(dve.tensor_tensor(ssum[:, :], p1[:, :], p2[:, :], ALU.add))
                    settle()
                    did(dve.reciprocal(rsum[:, :], ssum[:, :]))
                    settle()
                    did(dve.tensor_tensor(gate[:, q, 0, :], p1[:, :], rsum[:, :], ALU.mult))
                    did(dve.tensor_tensor(gate[:, q, 1, :], p2[:, :], rsum[:, :], ALU.mult))
                    dve.wait_ge(rank_ps, q + 1)
                    did(dve.tensor_copy(tot[:, :, :], ps[7][:, P:2 * P].rearrange("p (e j) -> p e j", e=NE)))
                    settle()
                    did(dve.tensor_tensor_scan(cum[:, :, :].rearrange("p e j -> p (e j)"), one_col[:, 0:1].to_broadcast([P, NE * NJ]),
                                               tot[:, :, :].rearrange("p e j -> p (e j)"), 0.0,
                                               ALU.mult, ALU.add))
                    settle()
                    did(dve.tensor_tensor(cum[:, :, :], cum[:, :, :], tot[:, :, :], ALU.subtract))
                    settle()
                    did(dve.tensor_tensor(cnt[:, :], cum[:, :, NJ - 1], tot[:, :, NJ - 1], ALU.add))
                    settle()
                    did(dve.tensor_tensor(cnt[:, :], cnt[:, :], cum[:, :, 0], ALU.subtract))
                    settle()
                    did(dve.tensor_tensor(over[:, :, :], over_j(cnt[:, :]),
                                          step128[:, :].unsqueeze(1).to_broadcast([P, NE, NJ]), ALU.is_gt))
                    settle()
                    did(dve.tensor_reduce(ctile[:, :], over[:, :, :], AX, ALU.add))
                    settle()
                    did(dve.tensor_tensor_scan(tend[:, :], one_col[:, 0:1].to_broadcast([P, NE]), ctile[:, :], 0.0, ALU.mult, ALU.add))
                    settle()
                    did(dve.tensor_tensor(tbase[:, :], tend[:, :], ctile[:, :], ALU.subtract))
                    did(dve.tensor_tensor(past[:, :, :], tile_no[:, :].unsqueeze(2).to_broadcast([P, TILES, NE]),
                                          tend[:, :].unsqueeze(1).to_broadcast([P, TILES, NE]), ALU.is_ge))
                    settle()
                    did(dve.scalar_tensor_tensor(tbase[:, :], tbase[:, :], float(P), cum[:, :, 0],
                                                 ALU.mult, ALU.subtract))
                    did(dve.tensor_reduce(owners[:, 2:2 + TILES], past[:, :, :], AX, ALU.add))
                    dve.tensor_tensor(pos[:, :, :], ps[7][:, 0:P].rearrange("p (e j) -> p e j", e=NE),
                                      cum[:, :, :], ALU.add).then_inc(rank_read, 1)
                    settle()
                    dve.wait_ge(rank_read, q + 1)
                    own = owners[:, 2:2 + TILES]
                    did(dve.tensor_scalar(own, own, float(NE - 1), None, ALU.min))
                    did(dve.tensor_tensor(pos[:, :, :], pos[:, :, :], over_j(tbase[:, :]), ALU.add))
                    settle()
                    part = [owners[:, m:m + TRIO * TRIOS + 1:TRIO] for m in range(WIN)]
                    did(dve.tensor_copy(windows[:, :], part[0]))
                    for m in range(1, WIN):
                        settle()
                        did(dve.scalar_tensor_tensor(windows[:, :], part[m], float(NE ** m), windows[:, :],
                                                     ALU.mult, ALU.add))
                    settle()
                    did(dve.tensor_copy(windows_i[:, q, 0:TRIOS + 1], windows[:, :]))
                    for k, hit in enumerate((hit1, hit2)):
                        did(dve.tensor_tensor(key[:, :, :], hit[:, :, :],
                                              pos[:, :, :].rearrange("p e j -> p j e"), ALU.mult))
                        settle()
                        did(dve.tensor_reduce(posf[:, :], key[:, :, :], AX, ALU.add))
                        settle()
                        last = dve.tensor_copy(slot[:, q, k, :], posf[:, :])
                        if k == 0:
                            did(last)
                            settle()
                    last.then_inc(slots_ready, 1)
                    dve.wait_ge(slots_ready, q + 1)
                    if q == 1:
                        dve.wait_ge(split_act, 2)
                        dve.tensor_tensor(w1lo[:, :], stage1, w1hi[:, :].bitcast(fp32),
                                          ALU.subtract).then_inc(split_dve, 1)
                        dve.tensor_tensor(w2[:, :, 1, :], stage2.rearrange("p (n d) -> p n d", d=D),
                                          w2[:, :, 0, :].bitcast(fp32), ALU.subtract).then_inc(split_dve, 1)
                        dve.wait_ge(b1_s, 16)
                elif kind == "experts":
                    base = TILES * q

                    def row_lo(s, k):
                        dve.wait_ge(rowhi_ready, base + s + 1)
                        dve.tensor_tensor(rowTlo[:, k, :], ps[6][:, 0:P], rowThi[:, k, :].bitcast(fp32),
                                          ALU.subtract).then_inc(rowlo_ready, 1)

                    def add_b1(i, k, window):
                        dve.wait_ge(up_done, base + TRIO * i + k + 1)
                        dve.tensor_tensor(mid[:, k, :], ps[k][:, :], b1_all[:, ds(window[k], DM)],
                                          ALU.add).then_inc(mid_ready, 1)

                    def mid_lo(s, k):
                        dve.wait_ge(midhi_ready, base + s + 1)
                        dve.scalar_tensor_tensor(midlo[:, k, :], ps[3 + k][:, :], 0.0,
                                                 midhi[:, k, :].bitcast(fp32), ALU.max,
                                                 ALU.subtract).then_inc(midlo_ready, 1)

                    def take_down(s, k):
                        dve.wait_ge(down_done, base + s + 1)
                        dve.tensor_reduce(flat_made[:, ds(s * D, D)],
                                          ps[7][:, 0:2 * D].rearrange("p (a d) -> p d a", a=2),
                                          AX, ALU.add).then_inc(made_ready, 1)

                    def turn(i, k, window):
                        s = TRIO * i + k
                        row_lo(s + 1, (k + 1) % TRIO)
                        add_b1(i, k, window)
                        mid_lo(s - 1, (k + 2) % TRIO)
                        take_down(s - 2, (k + 1) % TRIO)

                    def next_window(i):
                        dve.reg_load(dve_window, windows_i[0:1, q, ds(i, 1)])

                    def window_now():
                        window = dve.snap(dve_window, min_val=0, max_val=NE ** WIN - 1)
                        return [dve.snap(((window >> (BITS * (k + 2))) & (NE - 1)) * DM) for k in range(TRIO)]

                    next_window(0)
                    window = window_now()
                    row_lo(0, 0)
                    row_lo(1, 1)
                    add_b1(0, 0, window)
                    row_lo(2, 2)
                    add_b1(0, 1, window)
                    mid_lo(0, 0)
                    if q > 0:
                        dve.wait_ge(made_out, 16 * STORES * q)
                    next_window(1)
                    turn(0, 2, window)
                    with dve.Fori(1, TRIOS - 1) as trio:
                        window = window_now()
                        turn(trio, 0, window)
                        turn(trio, 1, window)
                        next_window(trio + 1)
                        turn(trio, 2, window)
                    window = window_now()
                    turn(TRIOS - 1, 0, window)
                    turn(TRIOS - 1, 1, window)
                    add_b1(TRIOS - 1, 2, window)
                    mid_lo(TILES - 2, 1)
                    take_down(TILES - 3, 0)
                    mid_lo(TILES - 1, 2)
                    take_down(TILES - 2, 1)
                    take_down(TILES - 1, 2)
                elif kind == "combine":
                    if f == 1:
                        dve.wait_ge(att_x, NU * HALVES)
                    Xh = X[:, h * NJ:(h + 1) * NJ, :]
                    did(dve.tensor_tensor(Xh, Xh, over_blocks(bout_all[:, :], NJ), ALU.add))

                    def weigh(i):
                        dve.wait_ge(gathered[i], 16 * 2 * U * (q + 1))
                        for j in range(U * i, U * i + U):
                            did(dve.tensor_scalar(back[1][:, j, :], back[1][:, j, :], gate[:, q, 1, j:j + 1],
                                                  None, ALU.mult))
                        settle()
                        for j in range(U * i, U * i + U):
                            last = dve.scalar_tensor_tensor(back[0][:, j, :], back[0][:, j, :],
                                                            gate[:, q, 0, j:j + 1], back[1][:, j, :],
                                                            ALU.mult, ALU.add)
                        last.then_inc(src_ready, 1)

                    def add_out(i):
                        n = unit[ph, i]
                        dve.wait_ge(projected, n + 1)
                        Xu = X[:, h * NJ + U * i:h * NJ + U * i + U, :]
                        dve.scalar_tensor_tensor(Xu, blocks(ps[2 + n % 2][:, :]), 0.5, Xu,
                                                 ALU.mult, ALU.add).then_inc(x_added, 1)

                    weigh(0)
                    for i in range(1, NU):
                        weigh(i)
                        add_out(i - 1)
                    add_out(NU - 1)
                else:
                    layernorm(ph)
                    batches = NU // UPB

                    def biggest(b):
                        n = h * batches + b
                        dve.wait_ge(score_ready, UPB * (n + 1))
                        if n:
                            dve.wait_ge(weight_ready, n)
                        dve.tensor_reduce(negmax[:, :], score, AX, ALU.max, negate=True).then_inc(max_ready, 1)

                    def sums(b):
                        n, at = h * batches + b, b * T
                        dve.wait_ge(weight_ready, n + 1)
                        if n == 0:
                            dve.wait_ge(made_out, 16 * STORES * HALVES)
                        if n and b == 0:
                            dve.wait_ge(out_ps, NU * h)
                        did(dve.tensor_tensor(weighted, weight, aT[:, at:at + T], ALU.mult))
                        settle()
                        did(dve.tensor_tensor_scan(num[:, at:at + T], one_col[:, 0:1].to_broadcast([P, T]),
                                                   weighted, 0.0, ALU.mult, ALU.add))
                        if n:
                            dve.wait_ge(den_ps, n)
                        dve.tensor_tensor_scan(den, one_col[:, 0:1].to_broadcast([P, T]), weight, 0.0,
                                               ALU.mult, ALU.add).then_inc(num_ready, 1)

                    def invert(b):
                        n = h * batches + b
                        dve.wait_ge(den_ps, n + 1)
                        dve.reciprocal(rdenT[:, b, :], ps[b][:, 0:8]).then_inc(den_read, 1)
                        dve.wait_ge(den_read, n + 1)

                    def pre(i):
                        a = kind_unit[ph, i]
                        g = blocks(gate_out[:, a % 2, :])
                        dve.wait_ge(out_ps, a + 1)
                        rd = rdenT[:, i // UPB, U * (i % UPB):U * (i % UPB) + U].unsqueeze(2).to_broadcast([P, U, D])
                        did(dve.tensor_tensor(g, blocks(ps[6][:, :]), rd, ALU.mult))
                        settle()
                        dve.tensor_tensor(g, blocks(ps[7][:, :]), g, ALU.add).then_inc(out_read, 1)
                        dve.wait_ge(out_read, a + 1)
                        dve.tensor_tensor(g, g, over_blocks(bc_all[:, :], U), ALU.add).then_inc(pre_ready, 1)

                    def add_att(i):
                        a = kind_unit[ph, i]
                        dve.wait_ge(gate_ready, a + 1)
                        Xu = X[:, h * NJ + U * i:h * NJ + U * i + U, :]
                        dve.tensor_tensor(Xu, Xu, blocks(gate_out[:, a % 2, :]), ALU.add).then_inc(att_x, 1)

                    biggest(0)
                    for b in range(batches):
                        sums(b)
                        invert(b)
                        if b + 1 < batches:
                            biggest(b + 1)
                        for i in range(b * UPB, (b + 1) * UPB):
                            if i >= 2:
                                add_att(i - 2)
                                dve.wait_ge(att_x, kind_unit[ph, i - 2] + 1)
                            pre(i)
                    add_att(NU - 2)
                    add_att(NU - 1)

        @block.tensor
        def _(pe):
            def bank_free(n):
                kind, a = unit_kind[n]
                pe.wait_ge({"route": h_ready, "combine": x_added, "attention": tanh_ready}[kind], a + 1)

            def middle_free(m):
                kind, a = middle_kind[m]
                pe.wait_ge(hT_ready if kind == "route" else score_ready, a + 1)

            def transpose_unit(ph, i, src):
                n = unit[ph, i]
                pe.wait_ge(src_ready, n + 1)
                if n >= 2:
                    pe.wait_ge(turned_out, n - 1)
                for k in range(U):
                    last = pe.transpose(ps[n % 2][:, k * P:(k + 1) * P], src[:, U * i + k, :], ident[:, :])
                last.then_inc(turned, 1)

            def project(ph, i, weights):
                n = unit[ph, i]
                pe.wait_ge(turned_out, n + 1)
                if n >= 2:
                    bank_free(n - 2)
                for k in range(U):
                    last = pe.matmul(ps[2 + n % 2][:, k * D:(k + 1) * D], xT[:, n % 2, k * P:(k + 1) * P],
                                     weights[:, :], start=True, stop=True)
                last.then_inc(projected, 1)

            pe_window = pe.alloc_register("tensor_window")
            pe.wait_ge(consts, 16)
            pe.wait_ge(small_s, 16 * 13)
            for k in range(3):
                last = pe.transpose(ps[7][:, k * P:(k + 1) * P], araw[:, k, :], ident[:, :])
            last.then_inc(aw_turned, 1)
            pe.wait_ge(chain, 10)
            pe.wait_ge(aw_copied, 2)

            for ph in PLAN:
                kind, f, h = ph
                q = q_of(ph)
                if kind == "route":
                    if f == 1:
                        pe.wait_ge(out_read, NU * (h + 1))
                    for i in range(NU + 3):
                        if i < NU:
                            transpose_unit(ph, i, H[h])
                        if 1 <= i <= NU:
                            project(ph, i - 1, win)
                        if 2 <= i <= NU + 1:
                            m = middle[ph, i - 2]
                            pe.wait_ge(h_ready, kind_unit[ph, i - 2] + 1)
                            if m >= 2:
                                middle_free(m - 2)
                            for k in range(U):
                                last = pe.transpose(ps[4 + m % 2][:, k * P:(k + 1) * P],
                                                    H[h][:, U * (i - 2) + k, :], ident[:, :])
                            last.then_inc(hT_ps, 1)
                        if i >= 3:
                            m = middle[ph, i - 3]
                            pe.wait_ge(hT_ready, kind_unit[ph, i - 3] + 1)
                            if i == 3 and q > 0:
                                pe.wait_ge(lg_read, q)
                            for k in range(U):
                                at = (U * (i - 3) + k) * NE
                                last = pe.matmul(ps[6][:, at:at + NE], hT[:, m % 2, k * P:(k + 1) * P],
                                                 wg[:, :], start=True, stop=True)
                            last.then_inc(lg_ps, 1)
                    pe.wait_ge(hits_ready, q + 1)
                    if q > 0:
                        pe.wait_ge(rank_read, q)
                    flat_hits = hits[:, :, :].rearrange("p e j -> p (e j)")
                    pe.matmul(ps[7][:, 0:P], before[:, :], flat_hits, start=True, stop=True)
                    pe.matmul(ps[7][:, P:2 * P], ones_bf[:, :], flat_hits, start=True, stop=True
                              ).then_inc(rank_ps, 1)
                elif kind == "combine":
                    if h == 0:
                        pe.wait_ge(made_ready, TILES * HALVES * (f + 1))
                        pe.wait_ge(midlo_ready, TILES * HALVES * (f + 1))
                    for i in range(NU + 1):
                        if i < NU:
                            transpose_unit(ph, i, back[0])
                        if i >= 1:
                            project(ph, i - 1, wout)
                elif kind == "attention":
                    for i in range(NU + 2):
                        if i < NU:
                            transpose_unit(ph, i, H[h])
                        if 1 <= i <= NU:
                            n = unit[ph, i - 1]
                            pe.wait_ge(turned_out, n + 1)
                            bank_free(n - 2)
                            pe.matmul(ps[2 + n % 2][:, :], w1T[:, :], aT[:, (i - 1) * W:i * W],
                                      start=True, stop=True).then_inc(projected, 1)
                        if i >= 2:
                            m, a = middle[ph, i - 2], kind_unit[ph, i - 2]
                            pe.wait_ge(tanh_ready, a + 1)
                            middle_free(m - 2)
                            pe.matmul(ps[4 + m % 2][:, :], w2rep[:, :], hT[:, m % 2, :],
                                      start=True, stop=True).then_inc(score_ps, 1)
                    for b in range(NU // UPB):
                        n = h * (NU // UPB) + b
                        pe.wait_ge(num_ready, n + 1)
                        for k in range(T // P):
                            last = pe.matmul(ps[b][:, k:k + 1], den[0:1, k * P:(k + 1) * P], one1[:, :],
                                             start=True, stop=True)
                        last.then_inc(den_ps, 1)
                        for i in range(b * UPB, (b + 1) * UPB):
                            a = kind_unit[ph, i]
                            if a >= 1:
                                pe.wait_ge(out_read, a)
                            elif h == 0:
                                pe.wait_ge(rank_read, HALVES)
                            for k in range(U):
                                at = i * W + k * P
                                pe.matmul(ps[6][:, k * D:(k + 1) * D], num[:, at:at + P], wcT[:, 0, :],
                                          start=True, stop=True)
                                last = pe.matmul(ps[7][:, k * D:(k + 1) * D], aT[:, at:at + P], wcT[:, 1, :],
                                                 start=True, stop=True)
                            last.then_inc(out_ps, 1)
                    pe.wait_ge(den_read, (h + 1) * (NU // UPB))
                else:
                    base = TILES * q
                    if h == 0:
                        last_unit = unit[("route", f, HALVES - 1), NU - 1]
                        pe.wait_ge(turned_out, last_unit + 1)
                        pe.wait_ge(h_ready, NU * HALVES * (f + 1))
                        pe.wait_ge(hT_ready, NU * HALVES * (f + 1))
                        pe.wait_ge(rank_read, HALVES * (f + 1))
                        pe.wait_ge(split_dve, 2)
                    pe.wait_ge(slots_ready, HALVES * (f + 1))

                    def turn_row(i, k):
                        pe.wait_ge(rows_in[k], 16 * (q * STORES + 1) + 16 * i)
                        pe.transpose(ps[6][:, 0:P], rows[:, k, :], ident[:, :]).then_inc(row_turned, 1)

                    def up(s, k, window):
                        e = window[0][k]
                        pe.matmul(ps[k][:, :], rowThi[:, k, :], w1hi[:, ds(e, DM)], start=True, stop=False)
                        pe.matmul(ps[k][:, :], rowThi[:, k, :], w1lo[:, ds(e, DM)], start=False, stop=False)
                        pe.matmul(ps[k][:, :], rowTlo[:, k, :], w1hi[:, ds(e, DM)], start=False, stop=True
                                  ).then_inc(up_done, 1)

                    def turn_mid(s, k):
                        pe.wait_ge(mid_ready, base + s + 1)
                        for c in range(NC):
                            last = pe.transpose(ps[3 + k][:, c * P:(c + 1) * P], mid[:, k, c * P:(c + 1) * P],
                                                ident[:, :])
                        last.then_inc(mid_turned, 1)

                    def down(s, k, window, m):
                        e = window[1][m]
                        pe.wait_ge(midlo_ready, base + s + 1)
                        if q > 0 or not isinstance(s, int) or s > 0:
                            pe.wait_ge(made_ready, base + s)
                        both, first = ps[7][:, 0:2 * D], ps[7][:, 0:D]
                        for c in range(NC):
                            at = e + c * 2 * D
                            pe.matmul(both, midhi[:, k, c * P:(c + 1) * P], flat_w2[:, ds(at, 2 * D)],
                                      start=c == 0, stop=False)
                            pe.matmul(first, midlo[:, k, c * P:(c + 1) * P], flat_w2[:, ds(at, D)],
                                      start=False, stop=False)
                        pe.matmul(first, ones2[:, :], b2_pair[:, ds(window[2][m], D)], start=False, stop=True
                                  ).then_inc(down_done, 1)

                    def turn(i, k, window):
                        s = TRIO * i + k
                        pe.wait_ge(rowlo_ready, base + s + 1)
                        turn_row(i + (k + 1) // TRIO, (k + 1) % TRIO)
                        up(s, k, window)
                        turn_mid(s - 1, (k + 2) % TRIO)
                        down(s - 2, (k + 1) % TRIO, window, k)

                    def next_window(i):
                        pe.reg_load(pe_window, windows_i[0:1, q, ds(i, 1)])

                    def window_now():
                        window = pe.snap(pe_window, min_val=0, max_val=NE ** WIN - 1)
                        expert = [pe.snap((window >> (BITS * m)) & (NE - 1)) for m in range(WIN)]
                        return ([pe.snap(expert[k + 2] * DM) for k in range(TRIO)],
                                [pe.snap(expert[m] * (NC * 2 * D)) for m in range(TRIO)],
                                [pe.snap(expert[m] * D) for m in range(TRIO)])

                    next_window(0)
                    window = window_now()
                    turn_row(0, 0)
                    pe.wait_ge(rowlo_ready, base + 1)
                    turn_row(0, 1)
                    up(0, 0, window)
                    pe.wait_ge(rowlo_ready, base + 2)
                    turn_row(0, 2)
                    up(1, 1, window)
                    turn_mid(0, 0)
                    next_window(1)
                    turn(0, 2, window)
                    with pe.Fori(1, TRIOS - 1) as trio:
                        window = window_now()
                        turn(trio, 0, window)
                        turn(trio, 1, window)
                        next_window(trio + 1)
                        turn(trio, 2, window)
                    window = window_now()
                    turn(TRIOS - 1, 0, window)
                    turn(TRIOS - 1, 1, window)
                    next_window(TRIOS)
                    pe.wait_ge(rowlo_ready, base + TILES)
                    up(TILES - 1, 2, window)
                    turn_mid(TILES - 2, 1)
                    down(TILES - 3, 0, window, 2)
                    turn_mid(TILES - 1, 2)
                    window = window_now()
                    down(TILES - 2, 1, window, 0)
                    down(TILES - 1, 2, window, 1)


_INS = ['L0_attn_x', 'L0_attn_W1', 'L0_attn_b1', 'L0_attn_w2', 'L0_attn_b2', 'L0_attn_Wc', 'L0_attn_bc',
        'L0_ffn_W_in', 'L0_ffn_b_in', 'L0_ffn_W_gate', 'L0_ffn_b_gate', 'L0_ffn_W1', 'L0_ffn_b1',
        'L0_ffn_W2', 'L0_ffn_b2', 'L0_ffn_W_out', 'L0_ffn_b_out']


def kernel(**inputs):
    import numpy as np
    import concourse.bacc as bacc
    from concourse.bass_utils import run_bass_kernel_spmd

    nc = bacc.Bacc("TRN2", target_bir_lowering=False, num_devices=1)
    arrays, args = {}, []
    for name in _INS:
        a = np.ascontiguousarray(inputs[name])
        arrays[f"in_{name}"] = a
        args.append(nc.dram_tensor(f"in_{name}", a.shape, mybir.dt.from_np(a.dtype), kind="ExternalInput").ap())
    shape = arrays["in_L0_attn_x"].shape
    args.append(nc.dram_tensor("out_0", shape, mybir.dt.float32, kind="ExternalOutput").ap())
    build_program(nc, *args)
    r = run_bass_kernel_spmd(nc, [arrays], core_ids=[0])
    return r.results[0]["out_0"]
```

```python
from contextlib import ExitStack

import concourse.bass as bass
from concourse import mybir


def build_program(nc, x_in, a_w1, a_b1, a_w2, a_b2, a_wc, a_bc, f_win, f_bin, f_wg, f_bg,
                  f_w1, f_b1, f_w2, f_b2, f_wout, f_bout, out):
    fp32, fp32r, bf16, i32 = (mybir.dt.float32, mybir.dt.float32r, mybir.dt.bfloat16,
                              mybir.dt.int32)
    ALU, ACT, AX = mybir.AluOpType, mybir.ActivationFunctionType, mybir.AxisListType.X
    ds = bass.ds

    P = 128
    D = f_win.shape[0]
    B, T = x_in.shape[0], x_in.shape[1]
    NE, _, DM = f_w1.shape
    NC = DM // P
    HALVES = 2
    NJ = B * T // P // HALVES
    U = 4
    NU = NJ // U
    UPB = T // P // U
    W = U * P
    TILES = 2 * NJ + NE - 1
    TRIO = 3
    STORES = TILES // TRIO
    EPS = 1e-5
    assert TILES % TRIO == 0 and D == P and NE == 8 and NU == 4 and UPB == 2

    PLAN = [("route", 0, 0), ("route", 0, 1), ("experts", 0, 0), ("experts", 0, 1),
            ("combine", 0, 0), ("attention", 0, 0), ("route", 1, 0),
            ("combine", 0, 1), ("attention", 0, 1), ("route", 1, 1),
            ("experts", 1, 0), ("experts", 1, 1), ("combine", 1, 0), ("combine", 1, 1)]
    BESIDE, COMBINED, NEXT = ("route", 1, 0), ("combine", 0, 1), ("attention", 0, 1)
    unit, kind_unit, middle, unit_kind, middle_kind = {}, {}, {}, [], []
    for ph in PLAN:
        if ph[0] != "experts":
            for i in range(NU):
                kind_unit[ph, i] = sum(k[0][0] == ph[0] for k in unit)
                middle[ph, i] = sum(k[0][0] != "combine" for k in unit)
                if ph[0] != "combine":
                    middle_kind.append((ph[0], kind_unit[ph, i]))
                unit[ph, i] = len(unit)
                unit_kind.append((ph[0], kind_unit[ph, i]))

    with ExitStack() as ctx:
        def sb(name, shape, dt=fp32):
            return ctx.enter_context(nc.sbuf_tensor(name, shape, dt))

        def sem(name):
            return ctx.enter_context(nc.semaphore(name))

        sorted_rows = [nc.dram_tensor(f"sorted_rows{h}", (TILES * P, D), fp32).ap() for h in range(HALVES)]
        expert_out = [nc.dram_tensor(f"expert_out{h}", (TILES * P, D), fp32).ap() for h in range(HALVES)]

        home = nc.dram_tensor("home", (P * TILES, 1), i32).ap()
        rows_home = nc.dram_tensor("rows_home", (2 * NJ * P + TILES * P, D), fp32).ap()

        X = sb("X", [P, HALVES * NJ, D])
        H = [sb(f"H{h}", [P, NJ, D]) for h in range(HALVES)]
        w1hi, w1lo = sb("w1hi", [P, NE * DM], fp32r), sb("w1lo", [P, NE * DM], fp32r)
        w2 = sb("w2", [P, NE * NC, 2, D], fp32r)
        flat_w2 = w2[:, :, :, :].rearrange("p n a d -> p (n a d)")
        b1_all = sb("b1_all", [P, NE * DM])
        pairs = sb("pairs", [2, (NE + 3) * D], fp32r)
        B_IN, B_2, B_OUT, B_C = 0, 1, NE + 1, NE + 2
        rows = sb("rows", [P, TILES, D])
        made = sb("made", [P, TILES, D])
        back = [sb(f"back{k}", [P, NJ, D]) for k in range(2)]
        midhi, midlo = sb("midhi", [P, TRIO, DM], fp32r), sb("midlo", [P, TRIO, DM], fp32r)
        rowThi, rowTlo = sb("rowThi", [P, TRIO, P], fp32r), sb("rowTlo", [P, TRIO, P], fp32r)
        turned_buf = sb("turned_buf", [P, 4, W])
        xT = turned_buf[:, 0:2, :]
        hT = turned_buf[:, 2:4, :]
        mid = turned_buf[:, 0:TRIO, :]
        araw = hT[:, 0, 0:3 * D].rearrange("p (a k) -> p a k", a=3)
        braw = H[1][0:2, 0:NE + 3, :].rearrange("p e d -> p (e d)")
        bhi = midhi[0:2, :, :].rearrange("p a k -> p (a k)")[:, 0:(NE + 3) * D]
        flat_rows = rows[:, :, :].rearrange("p t d -> p (t d)")
        flat_made = made[:, :, :].rearrange("p t d -> p (t d)")
        aT = flat_rows[:, 0:NU * W]
        gate_out = flat_made[:, 0:2 * W].rearrange("p (s w) -> p s w", s=2)
        stage1, stage2 = flat_rows[:, 0:NE * DM], flat_made[:, 0:NE * NC * D]

        win, wout, w1T = sb("win", [P, D]), sb("wout", [P, D]), sb("w1T", [P, D])
        wcT = sb("wcT", [P, 2, D])
        w2rep, w2col = sb("w2rep", [P, P]), sb("w2col", [P, 1])
        wg = sb("wg", [P, NE])
        bg_all = sb("bg_all", [P, NE])
        ab1, ab2 = sb("ab1", [P, 1]), sb("ab2", [P, 1])
        row_sel, row_not = sb("row_sel", [2, 1]), sb("row_not", [2, 1])
        ident = sb("ident", [P, P])
        before, ones_bf = sb("before", [P, P], bf16), sb("ones_bf", [P, P], bf16)
        ones2f, ones2 = sb("ones2f", [2, P]), sb("ones2", [2, P], fp32r)
        upto = sb("upto", [P, 2 * P])
        one_col = sb("one_col", [P, 1])
        rev_i, rev = sb("rev_i", [P, NE], i32), sb("rev", [P, NE])
        step_i, step128 = sb("step_i", [P, NJ], i32), sb("step128", [P, NJ])
        tile_i, tile_no = sb("tile_i", [P, TILES], i32), sb("tile_no", [P, TILES])
        stats, mv = sb("stats", [P, NJ, 6]), sb("mv", [P, NJ, 2])
        vare, std, rstd = sb("vare", [P, NJ]), sb("std", [P, NJ]), sb("rstd", [P, NJ])
        SMALL = NJ * NE
        lg, lg2, key, hit1, hit2, ex, tmp = (
            flat_rows[:, NU * W + 2 * T + n * SMALL:NU * W + 2 * T + (n + 1) * SMALL
                      ].rearrange("p (j e) -> p j e", e=NE) for n in range(7))
        tot, cum, pos, over = (
            flat_made[:, NU * W + 2 * T + n * SMALL:NU * W + 2 * T + (n + 1) * SMALL
                      ].rearrange("p (e j) -> p e j", e=NE) for n in range(4))
        best, kbest = sb("best", [P, NJ]), sb("kbest", [P, NJ])
        ssum, rsum, p1, p2 = sb("ssum", [P, NJ]), sb("rsum", [P, NJ]), sb("p1", [P, NJ]), sb("p2", [P, NJ])
        hits = sb("hits", [P, NE, NJ], bf16)
        cnt, ctile, tend, tbase = sb("cnt", [P, NE]), sb("ctile", [P, NE]), sb("tend", [P, NE]), sb("tbase", [P, NE])
        past = flat_made[:, NU * W + 2 * T + 4 * SMALL:NU * W + 2 * T + 4 * SMALL + TILES * NE].rearrange(
            "p (t e) -> p t e", e=NE)
        posf = sb("posf", [P, 2, NJ])
        NQ = 2 * HALVES
        TRIOS = TILES // TRIO
        owners = sb("owners", [P, TILES])
        w1_at = sb("w1_at", [P, NQ, TILES], i32)
        slot = sb("slot", [P, NQ, 2, NJ], i32)
        home_of, home_slot = sb("home_of", [P, 2, NJ], i32), sb("home_slot", [P, 2, NJ], i32)
        home_tile = sb("home_tile", [P, 2, NJ], i32)
        homes = sb("homes", [P, TILES], i32)
        gate = sb("gate", [P, NQ, 2, NJ])
        NB = NU // UPB
        tok_score, tok_weight, block_sum, block_cum, rden = (
            flat_rows[:, NU * W + n * NJ:NU * W + (n + 1) * NJ] for n in range(5))
        maxima = flat_rows[:, NU * W + 5 * NJ:NU * W + 6 * NJ]
        unit_max, big = maxima[:, 0:NU], maxima[:, NU:NU + NB]

        ps = [ctx.enter_context(nc.psum_tensor(f"bank{i}", [P, 512], fp32)) for i in range(8)]

        OUT_BANKS = [(0, 1), (6, 7)]

        x_in_s = [sem(f"x_loaded{c}") for c in range(4)]
        weights_s, small_s, b1_s = sem("expert_weights_loaded"), sem("small_loaded"), sem("b1_loaded")
        w2_s = sem("w2_loaded")
        consts = sem("constants_made")
        zeroed = sem("back_zeroed")
        rows_zero = [sem(f"sorted_rows{h}_zeroed") for h in range(HALVES)]
        split_act, split_dve = sem("weights_hi"), sem("weights_lo")
        aw_turned, aw_copied = sem("attention_weights_turned"), sem("attention_weights_copied")
        chain = sem("vector_step")
        var_ready, std_ready = sem("variance_ready"), sem("std_ready")
        src_ready, turned, turned_out = sem("unit_source_ready"), sem("unit_turned"), sem("unit_copied")
        projected = sem("unit_projected")
        h_ready, x_added, tanh_ready = sem("experts_input_ready"), sem("x_updated"), sem("hidden_ready")
        hT_ps, hT_ready, lg_ps = sem("h_turned"), sem("hT_copied"), sem("logits_done")
        lg_read, ex_in, ex_ready = sem("logits_read"), sem("exp_input"), sem("exp_done")
        hits_ready, rank_ps, rank_read = sem("hits_ready"), sem("ranks_done"), sem("ranks_read")
        slots_ready, owners_ready, gates_ready = sem("slots_ready"), sem("owners_ready"), sem("gates_ready")
        taken_up = [sem(f"taken_up{i}") for i in range(NU)]
        gated = sem("rows_times_gate")
        home_made, home_reset = sem("home_constants_made"), sem("home_reset")
        home_step, home_sent, homes_in, went_home = (sem("home_places"), sem("home_sent"), sem("homes_loaded"),
                                                     sem("rows_went_home"))
        scattered = [sem(f"scattered{h}") for h in range(HALVES)]
        rows_in = [sem(f"rows_loaded{k}") for k in range(TRIO)]
        made_out = sem("made_stored")
        row_turned, rowhi_ready, rowlo_ready = sem("tile_turned"), sem("tile_hi"), sem("tile_lo")
        up_done, mid_ready, mid_turned = sem("up_done"), sem("mid_ready"), sem("mid_turned")
        midhi_ready, midlo_ready = sem("mid_hi"), sem("mid_lo")
        down_done, made_ready = sem("down_done"), sem("tile_made")
        gathered = [sem(f"gathered{i}") for i in range(NU)]
        prep_ready = sem("bias_pairs_ready")
        score_ps, score_max, exp_in, weight_ready = (sem("scores_done"), sem("unit_max_taken"),
                                                     sem("token_scores_ready"), sem("token_weights_ready"))
        weighted_ready, num_ps, num_out = sem("weighted_rows_ready"), sem("sums_done"), sem("sums_copied")
        out_ps, out_read = sem("attention_out_done"), sem("attention_out_read")
        gate_ready, att_x = sem("tanh_output"), sem("attention_added")
        den_ps, den_read = sem("denominators_turned"), sem("denominators_read")
        stored = sem("out_stored")

        block = ctx.enter_context(nc.Block())

        def wait_rows_back(eng, q, i):
            if q < 2 * HALVES - 1:
                eng.wait_ge(gathered[i], 16 * 2 * U * (q + 1))
            else:
                eng.wait_ge(taken_up[i], 16 * 2)

        def q_of(ph):
            return ph[1] * HALVES + ph[2]

        def hT_used(eng, m):
            kind, a = middle_kind[m]
            eng.wait_ge(lg_ps if kind == "route" else score_ps, a + 1)

        x_rows = x_in.rearrange("b t d -> (b t) d").rearrange("(j p) d -> p j d", p=P)
        out_rows = out.rearrange("b t d -> (b t) d").rearrange("(j p) d -> p j d", p=P)

        SMALLS = 13

        @block.sync
        def _(sp):
            for c in range(4):
                sp.dma_start(X[:, 8 * c:8 * c + 8, :], x_rows[:, 8 * c:8 * c + 8, :]).then_inc(x_in_s[c], 16)
            sp.wait_ge(small_s, 16 * SMALLS)
            sp.wait_ge(zeroed, 2)

            def zero_rows(h):
                by_partition = sorted_rows[h].rearrange("(p r) d -> p r d", p=P)
                for k, (r0, n) in enumerate(((0, NJ), (NJ, NJ), (2 * NJ, TILES - 2 * NJ))):
                    sp.dma_start(by_partition[:, r0:r0 + n, :], back[k % 2][:, 0:n, :]).then_inc(rows_zero[h], 16)

            zero_rows(0)
            sp.wait_ge(home_made, 2)
            sp.dma_start(home.rearrange("(p t) a -> p (t a)", p=P), homes[:, :]).then_inc(home_reset, 16)
            sp.dma_start(stage1.rearrange("p (e m) -> p e m", e=NE),
                         f_w1.rearrange("e d m -> d e m")).then_inc(weights_s, 16)
            sp.dma_start(stage2.rearrange("p (e c d) -> p e c d", e=NE, c=NC),
                         f_w2.rearrange("e (c p) d -> p e c d", p=P)).then_inc(w2_s, 16)
            sp.dma_start(b1_all[:, :], f_b1.rearrange("e m -> (e m)").partition_broadcast(P)).then_inc(b1_s, 16)
            zero_rows(1)
            for ph in PLAN:
                kind, f, h = ph
                q = q_of(ph)
                if kind == "experts":
                    sp.wait_ge(scattered[h], 16 * 2 * NJ * (f + 1))
                    if f == 0 and h == 0:
                        sp.wait_ge(split_dve, 2)
                    if f == 1 and h == 0:
                        sp.wait_ge(att_x, 2 * NU)
                        sp.wait_ge(owners_ready, 2 * HALVES)
                    base, trios = TILES * q, TILES // TRIO

                    def load(i):
                        for k in range(TRIO):
                            if q > 0 or not isinstance(i, int) or i > 0:
                                sp.wait_ge(row_turned, base + TRIO * i + k - TRIO + 1)
                            sp.dma_start(rows[:, k, :], sorted_rows[h][ds((TRIO * i + k) * P, P), :]
                                         ).then_inc(rows_in[k], 16)

                    def store(i):
                        sp.wait_ge(made_ready, base + TRIO * i + TRIO)
                        sp.dma_start(expert_out[h][ds(TRIO * i * P, TRIO * P), :].rearrange("(t p) d -> p t d", p=P),
                                     made[:, ds(TRIO * i, TRIO), :]).then_inc(made_out, 16)

                    if q == 2 * HALVES - 1:
                        sp.wait_ge(home_sent, 16 * 2 * NJ)
                        sp.dma_start(homes[:, :], home.rearrange("(p t) a -> p (t a)", p=P)).then_inc(homes_in, 16)
                    load(0)
                    load(1)
                    with sp.Fori(2, trios) as trio:
                        load(trio)
                        if q < 2 * HALVES - 1:
                            store(trio - 2)
                    if q < 2 * HALVES - 1:
                        store(trios - 2)
                        store(trios - 1)
                if q == 2 * HALVES - 1 and kind == "experts":
                    sp.wait_ge(went_home, 16 * TILES)
                    for i in range(NU):
                        sp.wait_ge(turned, unit[("combine", 1, 0), i] + 1)
                        for k in range(2):
                            at = (k * NJ + U * i) * P
                            sp.dma_start(back[k][:, U * i:U * i + U, :], rows_home[at:at + U * P, :].rearrange(
                                "(j p) d -> p j d", p=P)).then_inc(taken_up[i], 16)
                if kind == "combine" and f == 1:
                    for i in range(NU):
                        sp.wait_ge(x_added, kind_unit[ph, i] + 1)
                        j = h * NJ + U * i
                        sp.dma_start(out_rows[:, j:j + U, :], X[:, j:j + U, :]).then_inc(stored, 16)
            sp.wait_ge(stored, 16 * HALVES * NU)

        @block.gpsimd
        def _(pool):
            pool.memset(back[0][:, :, :], 0.0).then_inc(zeroed, 1)
            pool.memset(back[1][:, :, :], 0.0).then_inc(zeroed, 1)
            pool.memset(ident[:, :], 0.0).then_inc(consts, 1)
            pool.memset(before[:, :], 1.0).then_inc(consts, 1)
            pool.memset(ones_bf[:, :], 1.0).then_inc(consts, 1)
            pool.memset(ones2f[:, :], 1.0).then_inc(consts, 1)
            pool.memset(upto[:, :], 1.0).then_inc(consts, 1)
            pool.memset(one_col[:, :], 1.0).then_inc(consts, 1)
            pool.memset(row_sel[:, :], 0.0).then_inc(consts, 1)
            pool.memset(row_not[:, :], 1.0).then_inc(consts, 1)
            pool.wait_ge(consts, 8)
            pool.affine_select(out=ident[:, :], in_=ident[:, :], compare_op=ALU.not_equal, fill=1.0, base=0,
                               pattern=[[-1, P]], channel_multiplier=1).then_inc(consts, 1)
            pool.affine_select(out=before[:, :], in_=before[:, :], compare_op=ALU.is_gt, fill=0.0, base=0,
                               pattern=[[1, P]], channel_multiplier=-1).then_inc(consts, 1)
            pool.affine_select(out=upto[:, 0:P], in_=upto[:, 0:P], compare_op=ALU.is_ge, fill=0.0, base=0,
                               pattern=[[1, P]], channel_multiplier=-1).then_inc(consts, 1)
            pool.affine_select(out=row_sel[:, :], in_=row_sel[:, :], compare_op=ALU.not_equal, fill=1.0, base=0,
                               pattern=[[0, 1]], channel_multiplier=1).then_inc(consts, 1)
            pool.affine_select(out=row_not[:, :], in_=row_not[:, :], compare_op=ALU.not_equal, fill=0.0, base=0,
                               pattern=[[0, 1]], channel_multiplier=1).then_inc(consts, 1)
            pool.iota(home_of[:, :, :], pattern=[[NJ * P, 2], [P, NJ]], base=0, channel_multiplier=1
                      ).then_inc(home_made, 1)
            pool.iota(homes[:, :], pattern=[[P, TILES]], base=2 * NJ * P, channel_multiplier=1
                      ).then_inc(home_made, 1)
            pool.iota(rev_i[:, :], pattern=[[-1, NE]], base=NE, channel_multiplier=0).then_inc(consts, 1)
            pool.iota(step_i[:, :], pattern=[[P, NJ]], base=0, channel_multiplier=0).then_inc(consts, 1)
            pool.iota(tile_i[:, :], pattern=[[1, TILES]], base=0, channel_multiplier=0).then_inc(consts, 1)

            def scatter(f, h):
                q = f * HALVES + h
                if f == 0:
                    pool.wait_ge(rows_zero[h], 16 * 3)
                pool.wait_ge(slots_ready, q + 1)
                pool.wait_ge(h_ready, NU * (q + 1))
                if f == 1:
                    pool.wait_ge(row_turned, TILES * HALVES)
                for j in range(NJ):
                    for k in range(2):
                        pool.indirect_dma_start(
                            sorted_rows[h], bass.IndirectOffsetOnAxis(slot[:, q, k, j:j + 1], 0),
                            H[h][:, j, :], None).then_inc(scattered[h], 16)

            def gather(f, h):
                q = f * HALVES + h
                pool.wait_ge(made_out, 16 * STORES * (q + 1))
                for i in range(NU):
                    if q > 0:
                        last = ("combine", (q - 1) // HALVES, (q - 1) % HALVES)
                        pool.wait_ge(turned, unit[last, i] + 1)
                    for j in range(U * i, U * i + U):
                        for k in range(2):
                            pool.indirect_dma_start(
                                back[k][:, j, :], None, expert_out[h],
                                bass.IndirectOffsetOnAxis(slot[:, q, k, j:j + 1], 0)).then_inc(gathered[i], 16)

            def send_homes(q):
                pool.wait_ge(home_step, 3)
                pool.wait_ge(home_reset, 16)
                for k in range(2):
                    for j in range(NJ):
                        pool.indirect_dma_start(
                            home, bass.IndirectOffsetOnAxis(home_slot[:, k, j:j + 1], 0),
                            home_of[:, k, j:j + 1], None).then_inc(home_sent, 16)

            def go_home(q):
                pool.wait_ge(homes_in, 16)
                for t in range(TILES):
                    pool.wait_ge(made_ready, q * TILES + t + 1)
                    pool.indirect_dma_start(
                        rows_home, bass.IndirectOffsetOnAxis(homes[:, t:t + 1], 0),
                        made[:, t, :], None).then_inc(went_home, 16)

            scatter(0, 0)
            scatter(0, 1)
            gather(0, 0)
            gather(0, 1)
            scatter(1, 0)
            scatter(1, 1)
            send_homes(2 * HALVES - 1)
            gather(1, 0)
            go_home(2 * HALVES - 1)

        @block.scalar
        def _(act):
            for dst, src in ((win, f_win), (wout, f_wout), (wg, f_wg),
                             (bg_all, f_bg.partition_broadcast(P)),
                             (ab1, a_b1.rearrange("(p a) -> p a", a=1)),
                             (ab2, a_b2.partition_broadcast(P)),
                             (w2col, a_w2.rearrange("a p -> p a")),
                             (braw[:, B_2 * D:(B_2 + NE) * D], f_b2.rearrange("e d -> (e d)").partition_broadcast(2)),
                             (braw[:, B_IN * D:(B_IN + 1) * D], f_bin.partition_broadcast(2)),
                             (braw[:, B_OUT * D:(B_OUT + 1) * D], f_bout.partition_broadcast(2)),
                             (braw[:, B_C * D:(B_C + 1) * D], a_bc.partition_broadcast(2))):
                act.dma_start(dst[:, :], src).then_inc(small_s, 16)
            act.dma_start(araw[:, 0, :], a_w1).then_inc(small_s, 16)
            act.dma_start(araw[:, 1:3, :], a_wc.rearrange("p (a k) -> p a k", a=2)).then_inc(small_s, 16)

            def copy_unit(ph, i, dst):
                act.wait_ge(turned, unit[ph, i] + 1)
                act.activation(dst, ps[unit[ph, i] % 2][:, :], ACT.Copy).then_inc(turned_out, 1)

            def xT_of(ph, i):
                n = unit[ph, i]
                if n >= 2:
                    act.wait_ge(projected, n - 1)
                copy_unit(ph, i, xT[:, n % 2, :])

            def root(n):
                act.wait_ge(var_ready, n + 1)
                act.activation(std[:, :], vare[:, :], ACT.Sqrt).then_inc(std_ready, 1)

            def times_gate(ph, i):
                q = q_of(ph)
                act.wait_ge(gates_ready, q + 1)
                wait_rows_back(act, q, i)
                for j in range(U * i, U * i + U):
                    last = act.activation(back[1][:, j, :], back[1][:, j, :], ACT.Copy,
                                          scale=gate[:, q, 1, j:j + 1])
                last.then_inc(gated, 1)

            def exponents(q):
                act.wait_ge(ex_in, q + 1)
                act.activation(ex[:, :, :], tmp[:, :, :], ACT.Exp).then_inc(ex_ready, 1)

            act.wait_ge(aw_turned, 1)
            act.activation(w1T[:, :], ps[7][:, 0:D], ACT.Copy).then_inc(aw_copied, 1)
            act.activation(wcT[:, :, :], ps[7][:, D:3 * D], ACT.Copy).then_inc(aw_copied, 1)
            lns = 0
            for ph in PLAN:
                kind, f, h = ph
                q = q_of(ph)
                if kind == "route":
                    if q != 1:
                        root(lns)
                        lns += 1
                    for i in range(NU + 2):
                        if i < NU:
                            xT_of(ph, i)
                            if ph == BESIDE:
                                times_gate(COMBINED, i)
                        if q == 0 and i == NU:
                            root(lns)
                            lns += 1
                        if 1 <= i <= NU:
                            n = unit[ph, i - 1]
                            act.wait_ge(projected, n + 1)
                            act.activation(H[h][:, U * (i - 1):U * i, :],
                                           ps[2 + n % 2][:, :].rearrange("p (u d) -> p u d", u=U),
                                           ACT.Copy).then_inc(h_ready, 1)
                        if i >= 2:
                            m = middle[ph, i - 2]
                            act.wait_ge(hT_ps, kind_unit[ph, i - 2] + 1)
                            if m >= 2:
                                hT_used(act, m - 2)
                            act.activation(hT[:, m % 2, :], ps[4 + m % 2][:, :], ACT.Copy).then_inc(hT_ready, 1)
                    if q == 1:
                        exponents(0)
                        act.wait_ge(weights_s, 16)
                        act.activation(w1hi[:, :], stage1, ACT.Copy).then_inc(split_act, 1)
                        act.wait_ge(w2_s, 16)
                        act.activation(w2[:, :, 0, :], stage2.rearrange("p (n d) -> p n d", d=D), ACT.Copy
                                       ).then_inc(split_act, 1)
                    if q > 0:
                        exponents(q)
                elif kind == "combine":
                    if ph != COMBINED:
                        times_gate(ph, 0)
                    for i in range(NU):
                        if i + 1 < NU and ph != COMBINED:
                            times_gate(ph, i + 1)
                        xT_of(ph, i)
                elif kind == "attention":
                    root(lns)
                    lns += 1
                    def hidden(i):
                        n, m, a = unit[ph, i], middle[ph, i], kind_unit[ph, i]
                        act.wait_ge(projected, n + 1)
                        if m >= 2:
                            hT_used(act, m - 2)
                        act.activation(hT[:, m % 2, :], ps[2 + n % 2][:, :], ACT.Tanh,
                                       bias=ab1[:, :]).then_inc(tanh_ready, 1)

                    def copy_sums(i):
                        a = kind_unit[ph, i]
                        act.wait_ge(num_ps, a + 1)
                        if i >= 2:
                            act.wait_ge(out_ps, a - 1)
                        for k in range(U):
                            to, of = xT[:, i % 2, k * P:(k + 1) * P], ps[4 + i % 2][:, k * P:(k + 1) * P]
                            if i % UPB == 0 and k == 0:
                                act.activation(to, of, ACT.Copy).then_inc(num_out, 1)
                            else:
                                before_it = xT[:, i % 2, k * P - 1:k * P] if k else xT[:, (i - 1) % 2, W - 1:W]
                                act.wait_ge(num_out, U * a + k)
                                act.activation(to, of, ACT.Identity, bias=before_it).then_inc(num_out, 1)

                    def outs(i):
                        a = kind_unit[ph, i]
                        act.wait_ge(out_read, a + 1)
                        act.activation(gate_out[:, a % 2, :], gate_out[:, a % 2, :], ACT.Tanh).then_inc(gate_ready, 1)

                    for i in range(NU + 1):
                        if i < NU:
                            copy_unit(ph, i, aT[:, i * W:(i + 1) * W])
                        if i >= 1:
                            hidden(i - 1)
                    act.wait_ge(exp_in, h + 1)
                    for b in range(NB):
                        blocks_of = slice(b * U * UPB, (b + 1) * U * UPB)
                        act.activation(tok_weight[:, blocks_of], tok_score[:, blocks_of], ACT.Exp,
                                       bias=big[:, b:b + 1]).then_inc(weight_ready, 1)
                    copy_sums(0)
                    copy_sums(1)
                    for i in range(NU):
                        if i + 2 < NU:
                            copy_sums(i + 2)
                        outs(i)
                else:
                    base = TILES * q

                    def row_hi(s, k):
                        act.wait_ge(row_turned, base + s + 1)
                        act.activation(rowThi[:, k, :], ps[6][:, 0:P], ACT.Copy).then_inc(rowhi_ready, 1)

                    def mid_hi(s, k):
                        act.wait_ge(mid_turned, base + s + 1)
                        act.activation(midhi[:, k, :], ps[3 + k][:, :], ACT.Relu).then_inc(midhi_ready, 1)

                    def turn(s, k):
                        row_hi(s + 1, (k + 1) % TRIO)
                        mid_hi(s - 1, (k + 2) % TRIO)

                    row_hi(0, 0)
                    row_hi(1, 1)
                    row_hi(2, 2)
                    mid_hi(0, 0)
                    turn(2, 2)
                    with act.Fori(1, TILES // TRIO - 1) as trio:
                        for k in range(TRIO):
                            turn(trio * TRIO + k, k)
                    turn(TILES - 3, 0)
                    turn(TILES - 2, 1)
                    mid_hi(TILES - 2, 1)
                    mid_hi(TILES - 1, 2)

        @block.vector
        def _(dve):
            steps = [0]

            def did(ins):
                steps[0] += 1
                return ins.then_inc(chain, 1)

            def settle():
                dve.wait_ge(chain, steps[0])

            def over_e(ap):
                return ap.unsqueeze(2).to_broadcast([P, NJ, NE])

            def over_j(ap):
                return ap.unsqueeze(2).to_broadcast([P, NE, NJ])

            def over_blocks(ap, n):
                return ap.unsqueeze(1).to_broadcast([P, n, D])

            def blocks(ap):
                return ap.rearrange("p (u d) -> p u d", u=U)

            b1_at = [dve.alloc_register(f"b1_at{k}") for k in range(TRIO)]
            dve.wait_ge(consts, 16)
            did(dve.tensor_copy(rev[:, :], rev_i[:, :]))
            did(dve.tensor_copy(step128[:, :], step_i[:, :]))
            did(dve.tensor_copy(tile_no[:, :], tile_i[:, :]))
            did(dve.tensor_copy(ones2[:, :], ones2f[:, :]))

            def prepare_biases(first, last):
                raw, hi = braw[:, first * D:last * D], bhi[:, first * D:last * D]
                did(dve.tensor_copy(hi, raw))
                settle()
                did(dve.tensor_tensor(raw, raw, hi.bitcast(fp32), ALU.subtract))
                settle()
                did(dve.tensor_scalar(raw, raw, row_not[:, :], None, ALU.mult))
                settle()
                dve.scalar_tensor_tensor(pairs[:, first * D:last * D], hi.bitcast(fp32), row_sel[:, :], raw,
                                         ALU.mult, ALU.add).then_inc(prep_ready, 1)

            def unit_stats(h, i):
                for j in range(U * i, U * i + U):
                    did(dve.bn_stats(stats[:, j, :], X[:, h * NJ + j, :]))
                settle()
                for j in range(U * i, U * i + U):
                    did(dve.bn_aggr(mv[:, j, :], stats[:, j, :]))

            def layernorm(ph):
                kind, f, h = ph
                j0 = h * NJ
                n = layernorm.count
                layernorm.count += 1
                if kind == "route" and f == 0:
                    for i in range(NU):
                        if i % 2 == 0:
                            dve.wait_ge(x_in_s[2 * h + i // 2], 16)
                        unit_stats(h, i)
                settle()
                dve.tensor_scalar(vare[:, :], mv[:, :, 1], EPS, None, ALU.add).then_inc(var_ready, 1)
                dve.wait_ge(std_ready, n + 1)
                did(dve.reciprocal(rstd[:, :], std[:, :]))
                settle()
                if kind == "attention":
                    dve.wait_ge(scattered[h], 16 * 2 * NJ)
                if kind == "route" and f == 1:
                    att = ("attention", 0, h)
                    dve.wait_ge(turned, unit[att, NU - 1] + 1)
                for i in range(NU):
                    for j in range(U * i, U * i + U):
                        last = dve.tensor_scalar(H[h][:, j, :], X[:, j0 + j, :], mv[:, j, 0:1],
                                                 rstd[:, j:j + 1], ALU.subtract, ALU.mult)
                    last.then_inc(src_ready, 1)

            layernorm.count = 0

            def first_hit(values, hit):
                did(dve.tensor_reduce(best[:, :], values[:, :, :], AX, ALU.max))
                settle()
                did(dve.tensor_tensor(hit[:, :, :], values[:, :, :], over_e(best[:, :]), ALU.is_equal))
                settle()
                did(dve.tensor_tensor(key[:, :, :], hit[:, :, :], rev[:, :].unsqueeze(1).to_broadcast([P, NJ, NE]),
                                      ALU.mult))
                settle()
                did(dve.tensor_reduce(kbest[:, :], key[:, :, :], AX, ALU.max))
                settle()
                did(dve.tensor_tensor(hit[:, :, :], key[:, :, :], over_e(kbest[:, :]), ALU.is_equal))

            def weigh(ph, i):
                q = q_of(ph)
                wait_rows_back(dve, q, i)
                dve.wait_ge(gated, NU * q + i + 1)
                for j in range(U * i, U * i + U):
                    last = dve.scalar_tensor_tensor(back[0][:, j, :], back[0][:, j, :],
                                                    gate[:, q, 0, j:j + 1], back[1][:, j, :],
                                                    ALU.mult, ALU.add)
                last.then_inc(src_ready, 1)

            def add_out(ph, i):
                kind, f, h = ph
                n = unit[ph, i]
                dve.wait_ge(projected, n + 1)
                Xu = X[:, h * NJ + U * i:h * NJ + U * i + U, :]
                dve.scalar_tensor_tensor(Xu, blocks(ps[2 + n % 2][:, :]), 0.5, Xu,
                                         ALU.mult, ALU.add).then_inc(x_added, 1)
                if f == 0:
                    dve.wait_ge(x_added, kind_unit[ph, i] + 1)
                    unit_stats(h, i)

            def choose_experts(q):
                dve.wait_ge(lg_ps, NU * (q + 1))
                dve.tensor_tensor(lg[:, :, :], ps[6][:, 0:NJ * NE].rearrange("p (j e) -> p j e", e=NE),
                                  bg_all[:, :].unsqueeze(1).to_broadcast([P, NJ, NE]), ALU.add
                                  ).then_inc(lg_read, 1)
                dve.wait_ge(lg_read, q + 1)
                first_hit(lg, hit1)
                dve.tensor_tensor(tmp[:, :, :], lg[:, :, :], over_e(best[:, :]), ALU.subtract).then_inc(ex_in, 1)
                settle()
                did(dve.scalar_tensor_tensor(lg2[:, :, :], hit1[:, :, :], -3.0e38, lg[:, :, :],
                                             ALU.mult, ALU.add))
                settle()
                dve.wait_ge(ex_in, q + 1)
                first_hit(lg2, hit2)
                settle()
                dve.tensor_tensor(hits[:, :, :].rearrange("p e j -> p j e"), hit1[:, :, :], hit2[:, :, :],
                                  ALU.add).then_inc(hits_ready, 1)

            def weigh_experts(q):
                dve.wait_ge(ex_ready, q + 1)
                did(dve.tensor_reduce(ssum[:, :], ex[:, :, :], AX, ALU.add))
                did(dve.tensor_tensor(tmp[:, :, :], ex[:, :, :], hit1[:, :, :], ALU.mult))
                did(dve.tensor_tensor(key[:, :, :], ex[:, :, :], hit2[:, :, :], ALU.mult))
                settle()
                did(dve.reciprocal(rsum[:, :], ssum[:, :]))
                did(dve.tensor_reduce(p1[:, :], tmp[:, :, :], AX, ALU.add))
                did(dve.tensor_reduce(p2[:, :], key[:, :, :], AX, ALU.add))
                settle()
                did(dve.tensor_tensor(p1[:, :], p1[:, :], rsum[:, :], ALU.mult))
                did(dve.tensor_tensor(p2[:, :], p2[:, :], rsum[:, :], ALU.mult))
                settle()
                did(dve.tensor_tensor(ssum[:, :], p1[:, :], p2[:, :], ALU.add))
                settle()
                did(dve.reciprocal(rsum[:, :], ssum[:, :]))
                settle()
                did(dve.tensor_tensor(gate[:, q, 0, :], p1[:, :], rsum[:, :], ALU.mult))
                dve.tensor_tensor(gate[:, q, 1, :], p2[:, :], rsum[:, :], ALU.mult).then_inc(gates_ready, 1)

            def place_rows(q):
                dve.wait_ge(rank_ps, q + 1)
                did(dve.tensor_copy(tot[:, :, :], ps[7][:, P:2 * P].rearrange("p (e j) -> p e j", e=NE)))
                settle()
                did(dve.tensor_reduce(cnt[:, :], tot[:, :, :], AX, ALU.add))
                did(dve.tensor_tensor_scan(cum[:, :, :].rearrange("p e j -> p (e j)"),
                                           one_col[:, 0:1].to_broadcast([P, NE * NJ]),
                                           tot[:, :, :].rearrange("p e j -> p (e j)"), 0.0, ALU.mult, ALU.add))
                settle()
                did(dve.tensor_tensor(over[:, :, :], over_j(cnt[:, :]),
                                      step128[:, :].unsqueeze(1).to_broadcast([P, NE, NJ]), ALU.is_gt))
                did(dve.tensor_tensor(cum[:, :, :], cum[:, :, :], tot[:, :, :], ALU.subtract))
                settle()
                did(dve.tensor_reduce(ctile[:, :], over[:, :, :], AX, ALU.add))
                dve.tensor_tensor(pos[:, :, :], ps[7][:, 0:P].rearrange("p (e j) -> p e j", e=NE),
                                  cum[:, :, :], ALU.add).then_inc(rank_read, 1)
                settle()
                did(dve.tensor_tensor_scan(tend[:, :], one_col[:, 0:1].to_broadcast([P, NE]), ctile[:, :], 0.0,
                                           ALU.mult, ALU.add))
                settle()
                did(dve.tensor_tensor(tbase[:, :], tend[:, :], ctile[:, :], ALU.subtract))
                settle()
                did(dve.scalar_tensor_tensor(tbase[:, :], tbase[:, :], float(P), cum[:, :, 0],
                                             ALU.mult, ALU.subtract))
                settle()
                dve.wait_ge(rank_read, q + 1)
                did(dve.tensor_tensor(pos[:, :, :], pos[:, :, :], over_j(tbase[:, :]), ALU.add))
                settle()
                places = pos[:, :, :].rearrange("p e j -> p j e")
                did(dve.tensor_tensor(key[:, :, :], hit1[:, :, :], places, ALU.mult))
                did(dve.tensor_tensor(lg2[:, :, :], hit2[:, :, :], places, ALU.mult))
                settle()
                did(dve.tensor_reduce(posf[:, 0, :], key[:, :, :], AX, ALU.add))
                did(dve.tensor_reduce(posf[:, 1, :], lg2[:, :, :], AX, ALU.add))
                settle()
                dve.tensor_copy(slot[:, q, :, :], posf[:, :, :]).then_inc(slots_ready, 1)
                did(dve.tensor_tensor(past[:, :, :], tile_no[:, :].unsqueeze(2).to_broadcast([P, TILES, NE]),
                                      tend[:, :].unsqueeze(1).to_broadcast([P, TILES, NE]), ALU.is_ge))
                settle()
                did(dve.tensor_reduce(owners[:, :], past[:, :, :], AX, ALU.add))
                settle()
                did(dve.tensor_scalar(owners[:, :], owners[:, :], float(NE - 1), float(DM), ALU.min, ALU.mult))
                settle()
                dve.tensor_copy(w1_at[:, q, :], owners[:, :]).then_inc(owners_ready, 1)
                dve.wait_ge(owners_ready, q + 1)

            for ph in PLAN:
                kind, f, h = ph
                q = q_of(ph)
                if kind == "route":
                    if q != 1:
                        layernorm(ph)
                    if q == 0:
                        dve.wait_ge(small_s, 16 * SMALLS)
                        prepare_biases(B_IN, B_IN + 1)
                        prepare_biases(B_2, B_C + 1)
                        did(dve.tensor_copy(w2rep[:, :], w2col[:, 0:1].to_broadcast([P, P])))
                        dve.wait_ge(prep_ready, 2)
                        layernorm(("route", 0, 1))
                    if ph == BESIDE:
                        for i in range(NU):
                            weigh(COMBINED, i)
                    choose_experts(q)
                    if ph == BESIDE:
                        for i in range(NU):
                            add_out(COMBINED, i)
                        layernorm(NEXT)
                    place_rows(q)
                    if q != 1 and q != 3:
                        weigh_experts(q)
                    if q == 2 * HALVES - 1:
                        dve.wait_ge(slots_ready, q + 1)
                        dve.tensor_scalar(home_tile[:, :, :], slot[:, q, :, :], 7, None, ALU.arith_shift_right
                                          ).then_inc(home_step, 1)
                        dve.tensor_scalar(home_slot[:, :, :], slot[:, q, :, :], P - 1, None, ALU.bitwise_and
                                          ).then_inc(home_step, 1)
                        dve.wait_ge(home_step, 2)
                        dve.scalar_tensor_tensor(home_slot[:, :, :], home_slot[:, :, :], float(TILES),
                                                 home_tile[:, :, :], ALU.mult, ALU.add).then_inc(home_step, 1)
                    if q == 1:
                        dve.wait_ge(split_act, 2)
                        dve.tensor_tensor(w1lo[:, :], stage1, w1hi[:, :].bitcast(fp32),
                                          ALU.subtract).then_inc(split_dve, 1)
                        dve.tensor_tensor(w2[:, :, 1, :], stage2.rearrange("p (n d) -> p n d", d=D),
                                          w2[:, :, 0, :].bitcast(fp32), ALU.subtract).then_inc(split_dve, 1)
                        dve.wait_ge(b1_s, 16)
                        weigh_experts(q)
                elif kind == "experts":
                    base = TILES * q

                    seen = {m: dve.alloc_register(f"seen{m + 1}_{q}") for m in range(-1, TRIO + 2)}

                    def count(s, m):
                        return seen[s[1] + m] if isinstance(s, tuple) else base + s + m

                    def row_lo(s, k):
                        dve.wait_ge(rowhi_ready, count(s, 2))
                        dve.tensor_tensor(rowTlo[:, k, :], ps[6][:, 0:P], rowThi[:, k, :].bitcast(fp32),
                                          ALU.subtract).then_inc(rowlo_ready, 1)

                    def add_b1(s, k, at):
                        dve.wait_ge(up_done, count(s, 1))
                        dve.tensor_tensor(mid[:, k, :], ps[k][:, :], b1_all[:, ds(at, DM)],
                                          ALU.add).then_inc(mid_ready, 1)

                    def mid_lo(s, k):
                        dve.wait_ge(midhi_ready, count(s, 0))
                        dve.scalar_tensor_tensor(midlo[:, k, :], ps[3 + k][:, :], 0.0,
                                                 midhi[:, k, :].bitcast(fp32), ALU.max,
                                                 ALU.subtract).then_inc(midlo_ready, 1)

                    def take_down(s, k, tile):
                        dve.wait_ge(down_done, count(s, -1))
                        dve.tensor_reduce(flat_made[:, ds(tile * D, D)],
                                          ps[7][:, 0:2 * D].rearrange("p (a d) -> p d a", a=2),
                                          AX, ALU.add).then_inc(made_ready, 1)

                    def fetch(trio):
                        dve.reg_load(b1_at, w1_at[0:1, q, ds(trio * TRIO, TRIO)])

                    def turn(s, k, at, tile, next_trio=None):
                        row_lo(s, (k + 1) % TRIO)
                        add_b1(s, k, at)
                        if next_trio is not None:
                            fetch(next_trio)
                        mid_lo(s, (k + 2) % TRIO)
                        take_down(s, (k + 1) % TRIO, tile - 2)

                    def places():
                        return [dve.snap(b1_at[k], min_val=0, max_val=(NE - 1) * DM) for k in range(TRIO)]

                    fetch(0)
                    at = places()
                    row_lo(-1, 0)
                    row_lo(0, 1)
                    add_b1(0, 0, at[0])
                    row_lo(1, 2)
                    add_b1(1, 1, at[1])
                    mid_lo(1, 0)
                    if q > 0:
                        dve.wait_ge(made_out, 16 * STORES * q)
                    turn(2, 2, at[2], 2)
                    fetch(1)
                    for m in seen:
                        dve.reg_mov(seen[m], base + TRIO + m)
                    with dve.Fori(1, TRIOS - 1) as trio:
                        at = places()
                        for k in range(TRIO):
                            turn(("loop", k), k, at[k], trio * TRIO + k, trio + 1 if k == TRIO - 1 else None)
                        for m in seen:
                            dve.reg_add(seen[m], seen[m], TRIO)
                    at = places()
                    turn(TILES - 3, 0, at[0], TILES - 3)
                    turn(TILES - 2, 1, at[1], TILES - 2)
                    add_b1(TILES - 1, 2, at[2])
                    mid_lo(TILES - 1, 1)
                    take_down(TILES - 1, 0, TILES - 3)
                    mid_lo(TILES, 2)
                    take_down(TILES, 1, TILES - 2)
                    take_down(TILES + 1, 2, TILES - 1)
                    for m in seen:
                        dve.free_register(seen[m])
                elif kind == "combine":
                    if ph != COMBINED:
                        weigh(ph, 0)
                        weigh(ph, 1)
                        if f == 1 and h == 0:
                            weigh_experts(2 * HALVES - 1)
                        for i in range(NU):
                            if i + 2 < NU:
                                weigh(ph, i + 2)
                            add_out(ph, i)
                else:
                    if ph != NEXT:
                        layernorm(ph)
                    for i in range(NU):
                        m, a = middle[ph, i], kind_unit[ph, i]
                        dve.wait_ge(score_ps, a + 1)
                        dve.tensor_reduce(unit_max[:, i:i + 1], ps[4 + m % 2][:, :], AX, ALU.max
                                          ).then_inc(score_max, 1)
                    did(dve.tensor_scalar(tok_score[:, :], ps[7][:, 0:NJ], ab2[:, :], None, ALU.add))
                    dve.wait_ge(score_max, NU * (h + 1))
                    did(dve.tensor_reduce(big[:, :], unit_max[:, :].rearrange("p (b i) -> p b i", b=NB), AX, ALU.max))
                    settle()
                    dve.tensor_scalar(big[:, :], big[:, :], ab2[:, :], -1.0, ALU.add, ALU.mult).then_inc(exp_in, 1)
                    dve.wait_ge(turned, unit[ph, NU - 1] + 1)
                    dve.wait_ge(weight_ready, NB * (h + 1))
                    def weigh_rows(i):
                        for j in range(U * i, U * i + U):
                            last = dve.tensor_scalar(H[h][:, j, :], H[h][:, j, :], tok_weight[:, j:j + 1], None,
                                                     ALU.mult)
                        last.then_inc(weighted_ready, 1)

                    weigh_rows(0)
                    weigh_rows(1)
                    dve.wait_ge(den_ps, h + 1)
                    did(dve.tensor_copy(block_sum[:, :], ps[7][:, NJ:2 * NJ]))
                    settle()
                    for b in range(NB):
                        bs = slice(b * U * UPB, (b + 1) * U * UPB)
                        did(dve.tensor_tensor_scan(block_cum[:, bs], one_col[:, 0:1].to_broadcast([P, U * UPB]),
                                                   block_sum[:, bs], 0.0, ALU.mult, ALU.add))
                    settle()
                    did(dve.tensor_tensor(block_cum[:, :], block_cum[:, :], block_sum[:, :], ALU.subtract))
                    settle()
                    dve.tensor_tensor(block_cum[:, :], block_cum[:, :], ps[7][:, 0:NJ], ALU.add).then_inc(den_read, 1)
                    weigh_rows(2)
                    weigh_rows(3)
                    dve.wait_ge(den_read, h + 1)
                    did(dve.reciprocal(rden[:, :], block_cum[:, :]))
                    settle()
                    if h == 0:
                        dve.wait_ge(made_out, 16 * STORES * HALVES)

                    def pre(i):
                        a = kind_unit[ph, i]
                        g = blocks(gate_out[:, a % 2, :])
                        dve.wait_ge(out_ps, a + 1)
                        rd = rden[:, U * i:U * i + U].unsqueeze(2).to_broadcast([P, U, D])
                        did(dve.tensor_tensor(g, blocks(ps[OUT_BANKS[i % 2][0]][:, :]), rd, ALU.mult))
                        settle()
                        dve.tensor_tensor(g, blocks(ps[OUT_BANKS[i % 2][1]][:, :]), g, ALU.add).then_inc(out_read, 1)

                    def add_att(i):
                        a = kind_unit[ph, i]
                        dve.wait_ge(gate_ready, a + 1)
                        Xu = X[:, h * NJ + U * i:h * NJ + U * i + U, :]
                        dve.tensor_tensor(Xu, Xu, blocks(gate_out[:, a % 2, :]), ALU.add).then_inc(att_x, 1)
                        dve.wait_ge(att_x, a + 1)
                        unit_stats(h, i)

                    pre(0)
                    for i in range(1, NU):
                        pre(i)
                        add_att(i - 1)
                    add_att(NU - 1)

        @block.tensor
        def _(pe):
            def bank_free(n):
                kind, a = unit_kind[n]
                pe.wait_ge({"route": h_ready, "combine": x_added, "attention": tanh_ready}[kind], a + 1)

            def middle_free(m):
                kind, a = middle_kind[m]
                pe.wait_ge(hT_ready if kind == "route" else score_max, a + 1)

            def transpose_unit(ph, i, src):
                n = unit[ph, i]
                pe.wait_ge(src_ready, n + 1)
                if n >= 2:
                    pe.wait_ge(turned_out, n - 1)
                for k in range(U):
                    last = pe.transpose(ps[n % 2][:, k * P:(k + 1) * P], src[:, U * i + k, :], ident[:, :])
                last.then_inc(turned, 1)

            def bias_row(bank, which):
                pe.matmul(bank[:, :], ones2[:, :], pairs[:, which * D:(which + 1) * D].unsqueeze(1)
                          .to_broadcast([2, U, D]), start=True, stop=False)

            def project(ph, i, weights, which):
                pe.wait_ge(prep_ready, 1 if which == B_IN else 2)
                n = unit[ph, i]
                pe.wait_ge(turned_out, n + 1)
                if n >= 2:
                    bank_free(n - 2)
                bias_row(ps[2 + n % 2], which)
                for k in range(U):
                    last = pe.matmul(ps[2 + n % 2][:, k * D:(k + 1) * D], xT[:, n % 2, k * P:(k + 1) * P],
                                     weights[:, :], start=False, stop=k == U - 1)
                last.then_inc(projected, 1)

            def ranks(q):
                pe.wait_ge(hits_ready, q + 1)
                if q > 0:
                    pe.wait_ge(rank_read, q)
                flat_hits = hits[:, :, :].rearrange("p e j -> p (e j)")
                pe.matmul(ps[7][:, 0:P], before[:, :], flat_hits, start=True, stop=True)
                pe.matmul(ps[7][:, P:2 * P], ones_bf[:, :], flat_hits, start=True, stop=True
                          ).then_inc(rank_ps, 1)

            up_at = [pe.alloc_register(f"up_at{k}") for k in range(TRIO)]
            down_at = [pe.alloc_register(f"down_at{k}") for k in range(TRIO)]
            pe.wait_ge(consts, 16)
            pe.wait_ge(small_s, 16 * SMALLS)
            for k in range(3):
                last = pe.transpose(ps[7][:, k * P:(k + 1) * P], araw[:, k, :], ident[:, :])
            last.then_inc(aw_turned, 1)
            pe.wait_ge(aw_copied, 2)

            for ph in PLAN:
                kind, f, h = ph
                q = q_of(ph)
                if kind == "route":
                    if f == 1:
                        pe.wait_ge(out_read, NU * (h + 1))
                    for i in range(NU + 3):
                        if i < NU:
                            transpose_unit(ph, i, H[h])
                        if 1 <= i <= NU:
                            project(ph, i - 1, win, B_IN)
                        if 2 <= i <= NU + 1:
                            m = middle[ph, i - 2]
                            pe.wait_ge(h_ready, kind_unit[ph, i - 2] + 1)
                            if m >= 2:
                                middle_free(m - 2)
                            for k in range(U):
                                last = pe.transpose(ps[4 + m % 2][:, k * P:(k + 1) * P],
                                                    H[h][:, U * (i - 2) + k, :], ident[:, :])
                            last.then_inc(hT_ps, 1)
                        if i >= 3:
                            m = middle[ph, i - 3]
                            pe.wait_ge(hT_ready, kind_unit[ph, i - 3] + 1)
                            if i == 3 and q > 0:
                                pe.wait_ge(lg_read, q)
                            for k in range(U):
                                at = (U * (i - 3) + k) * NE
                                last = pe.matmul(ps[6][:, at:at + NE], hT[:, m % 2, k * P:(k + 1) * P],
                                                 wg[:, :], start=True, stop=True)
                            last.then_inc(lg_ps, 1)
                        if q == 1 and i == 1:
                            ranks(0)
                    if q > 0 and ph != BESIDE:
                        ranks(q)
                elif kind == "combine":
                    if h == 0:
                        pe.wait_ge(made_ready, TILES * HALVES * (f + 1))
                        pe.wait_ge(midlo_ready, TILES * HALVES * (f + 1))
                    for i in range(NU + 1):
                        if i < NU:
                            transpose_unit(ph, i, back[0])
                        if i >= 1:
                            project(ph, i - 1, wout, B_OUT)
                        if ph == COMBINED and i == 2:
                            ranks(q_of(BESIDE))
                elif kind == "attention":
                    for i in range(NU + 2):
                        if i < NU:
                            transpose_unit(ph, i, H[h])
                        if 1 <= i <= NU:
                            n = unit[ph, i - 1]
                            pe.wait_ge(turned_out, n + 1)
                            bank_free(n - 2)
                            pe.matmul(ps[2 + n % 2][:, :], w1T[:, :], aT[:, (i - 1) * W:i * W],
                                      start=True, stop=True).then_inc(projected, 1)
                        if i >= 2:
                            m, a = middle[ph, i - 2], kind_unit[ph, i - 2]
                            pe.wait_ge(tanh_ready, a + 1)
                            middle_free(m - 2)
                            pe.matmul(ps[4 + m % 2][:, :], w2rep[:, :], hT[:, m % 2, :],
                                      start=True, stop=True)
                            if i == 2:
                                pe.wait_ge(rank_read, HALVES + h)
                                if h:
                                    pe.wait_ge(out_read, NU * h)
                            for k in range(U):
                                at = U * (i - 2) + k
                                last = pe.matmul(ps[7][:, at:at + 1], hT[:, m % 2, k * P:(k + 1) * P], w2col[:, :],
                                                 start=True, stop=True)
                            last.then_inc(score_ps, 1)
                    pe.wait_ge(weight_ready, NB * (h + 1))
                    pe.matmul(ps[7][:, 0:NJ], upto[:, 0:P], tok_weight[:, :], start=True, stop=True)
                    pe.matmul(ps[7][:, NJ:2 * NJ], upto[:, P:2 * P], tok_weight[:, :], start=True, stop=True
                              ).then_inc(den_ps, 1)
                    pe.wait_ge(score_max, NU * (h + 1))
                    pe.wait_ge(turned_out, unit[ph, NU - 1] + 1)

                    def sums(i):
                        bank = ps[4 + i % 2]
                        pe.wait_ge(weighted_ready, NU * h + i + 1)
                        if i >= 2:
                            pe.wait_ge(num_out, U * (kind_unit[ph, i] - 1))
                        for k in range(U):
                            last = pe.matmul(bank[:, k * P:(k + 1) * P], H[h][:, U * i + k, :], upto[:, 0:P],
                                             start=True, stop=True)
                        last.then_inc(num_ps, 1)

                    def outs(i):
                        a = kind_unit[ph, i]
                        pe.wait_ge(num_out, U * (a + 1))
                        if i >= 2:
                            pe.wait_ge(out_read, a - 1)
                        if i == 1:
                            pe.wait_ge(den_read, h + 1)
                            pe.wait_ge(lg_read, HALVES + h)
                        of_sums, of_x = (ps[n] for n in OUT_BANKS[i % 2])
                        bias_row(of_x, B_C)
                        for k in range(U):
                            pe.matmul(of_sums[:, k * D:(k + 1) * D], xT[:, i % 2, k * P:(k + 1) * P],
                                      wcT[:, 0, :], start=True, stop=True)
                            last = pe.matmul(of_x[:, k * D:(k + 1) * D], aT[:, i * W + k * P:i * W + (k + 1) * P],
                                             wcT[:, 1, :], start=False, stop=k == U - 1)
                        last.then_inc(out_ps, 1)

                    sums(0)
                    sums(1)
                    for i in range(NU):
                        outs(i)
                        if i + 2 < NU:
                            sums(i + 2)
                    pe.wait_ge(out_read, NU * (h + 1))
                else:
                    base = TILES * q
                    if h == 0:
                        last_unit = unit[("route", f, HALVES - 1), NU - 1]
                        pe.wait_ge(turned_out, last_unit + 1)
                        pe.wait_ge(h_ready, NU * HALVES * (f + 1))
                        pe.wait_ge(hT_ready, NU * HALVES * (f + 1))
                        pe.wait_ge(rank_read, HALVES * (f + 1))
                        pe.wait_ge(split_dve, 2)
                    pe.wait_ge(owners_ready, HALVES * (f + 1))

                    seen = {m: pe.alloc_register(f"seen{m + 2}_{q}") for m in range(-2, TRIO + 2)}
                    loads_seen = pe.alloc_register(f"loads_seen_{q}")

                    def count(s, m):
                        return seen[s[1] + m] if isinstance(s, tuple) else base + s + m

                    def turn_row(loads, k):
                        pe.wait_ge(rows_in[k], loads)
                        pe.transpose(ps[6][:, 0:P], rows[:, k, :], ident[:, :]).then_inc(row_turned, 1)

                    def up(k, at):
                        pe.matmul(ps[k][:, :], rowThi[:, k, :], w1hi[:, ds(at, DM)], start=True, stop=False)
                        pe.matmul(ps[k][:, :], rowThi[:, k, :], w1lo[:, ds(at, DM)], start=False, stop=False)
                        pe.matmul(ps[k][:, :], rowTlo[:, k, :], w1hi[:, ds(at, DM)], start=False, stop=True
                                  ).then_inc(up_done, 1)

                    def turn_mid(s, k):
                        pe.wait_ge(mid_ready, count(s, 0))
                        for c in range(NC):
                            last = pe.transpose(ps[3 + k][:, c * P:(c + 1) * P], mid[:, k, c * P:(c + 1) * P],
                                                ident[:, :])
                        last.then_inc(mid_turned, 1)

                    def down(s, k, at):
                        pe.wait_ge(midlo_ready, count(s, -1))
                        if q > 0 or not s == 2:
                            pe.wait_ge(made_ready, count(s, -2))
                        both, first = ps[7][:, 0:2 * D], ps[7][:, 0:D]
                        for c in range(NC):
                            chunk = flat_w2[:, c * 2 * D:]
                            pe.matmul(both, midhi[:, k, c * P:(c + 1) * P], chunk[:, ds(at * 2, 2 * D)],
                                      start=c == 0, stop=False)
                            pe.matmul(first, midlo[:, k, c * P:(c + 1) * P], chunk[:, ds(at * 2, D)],
                                      start=False, stop=False)
                        pe.matmul(first, ones2[:, :], b2_of(at), start=False, stop=True).then_inc(down_done, 1)

                    def b2_of(at):
                        return pairs[:, B_2 * D:][:, ds(at // (DM // D), D)]

                    def row_and_up(s, k, at, loads):
                        pe.wait_ge(rowlo_ready, count(s, 1))
                        turn_row(loads, (k + 1) % TRIO)
                        up(k, at)

                    def fetch(trio):
                        pe.reg_load(up_at, w1_at[0:1, q, ds(trio * TRIO, TRIO)])

                    def keep():
                        for k in range(TRIO):
                            pe.reg_mov(down_at[k], up_at[k])

                    def places(registers):
                        return [pe.snap(reg, min_val=0, max_val=(NE - 1) * DM) for reg in registers]

                    first_load = 16 * (q * STORES + 1)
                    fetch(0)
                    at = places(up_at)
                    turn_row(first_load, 0)
                    row_and_up(0, 0, at[0], first_load)
                    row_and_up(1, 1, at[1], first_load)
                    turn_mid(1, 0)
                    row_and_up(2, 2, at[2], first_load + 16)
                    keep()
                    fetch(1)
                    for m in seen:
                        pe.reg_mov(seen[m], base + TRIO + m)
                    pe.reg_mov(loads_seen, first_load + 16)
                    turn_mid(2, 1)
                    down(2, 0, at[0])
                    row_and_up(3, 0, places(up_at)[0], first_load + 16)
                    with pe.Fori(1, TRIOS - 1) as trio:
                        at, before_at = places(up_at), places(down_at[1:])
                        turn_mid(("loop", 0), 2)
                        down(("loop", 0), 1, before_at[0])
                        row_and_up(("loop", 1), 1, at[1], loads_seen)
                        turn_mid(("loop", 1), 0)
                        down(("loop", 1), 2, before_at[1])
                        pe.reg_add(loads_seen, loads_seen, 16)
                        row_and_up(("loop", 2), 2, at[2], loads_seen)
                        keep()
                        fetch(trio + 1)
                        turn_mid(("loop", 2), 1)
                        down(("loop", 2), 0, at[0])
                        row_and_up(("loop", 3), 0, places(up_at)[0], loads_seen)
                        for m in seen:
                            pe.reg_add(seen[m], seen[m], TRIO)
                    at, before_at = places(up_at), places(down_at[1:])
                    last_load = first_load + 16 * (TRIOS - 1)
                    turn_mid(TILES - 3, 2)
                    down(TILES - 3, 1, before_at[0])
                    row_and_up(TILES - 2, 1, at[1], last_load)
                    turn_mid(TILES - 2, 0)
                    down(TILES - 2, 2, before_at[1])
                    pe.wait_ge(rowlo_ready, base + TILES)
                    up(2, at[2])
                    turn_mid(TILES - 1, 1)
                    down(TILES - 1, 0, at[0])
                    turn_mid(TILES, 2)
                    down(TILES, 1, at[1])
                    down(TILES + 1, 2, at[2])
                    for reg in (*seen.values(), loads_seen):
                        pe.free_register(reg)


_INS = ['L0_attn_x', 'L0_attn_W1', 'L0_attn_b1', 'L0_attn_w2', 'L0_attn_b2', 'L0_attn_Wc', 'L0_attn_bc',
        'L0_ffn_W_in', 'L0_ffn_b_in', 'L0_ffn_W_gate', 'L0_ffn_b_gate', 'L0_ffn_W1', 'L0_ffn_b1',
        'L0_ffn_W2', 'L0_ffn_b2', 'L0_ffn_W_out', 'L0_ffn_b_out']


def kernel(**inputs):
    import numpy as np
    import concourse.bacc as bacc
    from concourse.bass_utils import run_bass_kernel_spmd

    nc = bacc.Bacc("TRN2", target_bir_lowering=False, num_devices=1)
    arrays, args = {}, []
    for name in _INS:
        a = np.ascontiguousarray(inputs[name])
        arrays[f"in_{name}"] = a
        args.append(nc.dram_tensor(f"in_{name}", a.shape, mybir.dt.from_np(a.dtype), kind="ExternalInput").ap())
    shape = arrays["in_L0_attn_x"].shape
    args.append(nc.dram_tensor("out_0", shape, mybir.dt.float32, kind="ExternalOutput").ap())
    build_program(nc, *args)
    r = run_bass_kernel_spmd(nc, [arrays], core_ids=[0])
    return r.results[0]["out_0"]
```

```python
from contextlib import ExitStack

import concourse.bass as bass
from concourse import mybir


def build_program(nc, x_in, a_w1, a_b1, a_w2, a_b2, a_wc, a_bc, f_win, f_bin, f_wg, f_bg,
                  f_w1, f_b1, f_w2, f_b2, f_wout, f_bout, out):
    fp32, fp32r, bf16, i32 = (mybir.dt.float32, mybir.dt.float32r, mybir.dt.bfloat16,
                              mybir.dt.int32)
    ALU, ACT, AX = mybir.AluOpType, mybir.ActivationFunctionType, mybir.AxisListType.X
    ds = bass.ds

    P = 128
    D = f_win.shape[0]
    B, T = x_in.shape[0], x_in.shape[1]
    NE, _, DM = f_w1.shape
    NC = DM // P
    HALVES = 2
    NJ = B * T // P // HALVES
    U = 4
    NU = NJ // U
    UPB = T // P // U
    W = U * P
    TILES = 2 * NJ + NE - 1
    TRIO = 3
    STORES = TILES // TRIO
    EPS = 1e-5
    assert TILES % TRIO == 0 and D == P and NE == 8 and NU == 4 and UPB == 2
    assert NE * DM == NE * NC * D and NU * W + 6 * NJ <= NE * DM

    PLAN = [("route", 0, 0), ("route", 0, 1), ("experts", 0, 0),
            ("combine", 0, 0), ("attention", 0, 0), ("combine", 0, 1), ("route", 1, 0),
            ("attention", 0, 1), ("route", 1, 1),
            ("experts", 1, 0), ("combine", 1, 0), ("combine", 1, 1)]
    COMBINED, ROUTED, BESIDE = ("combine", 0, 1), ("route", 1, 0), ("attention", 0, 1)
    unit, kind_unit, middle, unit_kind, middle_kind = {}, {}, {}, [], []
    for ph in PLAN:
        if ph[0] != "experts":
            for i in range(NU):
                kind_unit[ph, i] = sum(k[0][0] == ph[0] for k in unit)
                middle[ph, i] = sum(k[0][0] != "combine" for k in unit)
                if ph[0] != "combine":
                    middle_kind.append((ph[0], kind_unit[ph, i]))
                unit[ph, i] = len(unit)
                unit_kind.append((ph[0], kind_unit[ph, i]))

    with ExitStack() as ctx:
        def sb(name, shape, dt=fp32):
            return ctx.enter_context(nc.sbuf_tensor(name, shape, dt))

        def sem(name):
            return ctx.enter_context(nc.semaphore(name))

        sorted_rows = [nc.dram_tensor(f"sorted_rows{h}", (TILES * P, D), fp32).ap() for h in range(HALVES)]
        expert_out = [nc.dram_tensor(f"expert_out{h}", (TILES * P, D), fp32).ap() for h in range(HALVES)]

        home = nc.dram_tensor("home", (P * TILES, 1), i32).ap()
        rows_home = nc.dram_tensor("rows_home", (2 * NJ * P + TILES * P, D), fp32).ap()

        X = sb("X", [P, HALVES * NJ, D])
        H = [sb(f"H{h}", [P, NJ, D]) for h in range(HALVES)]
        w1hi, w1lo = sb("w1hi", [P, NE * DM], fp32r), sb("w1lo", [P, NE * DM], fp32r)
        w2 = sb("w2", [P, NE * NC, 2, D], fp32r)
        flat_w2 = w2[:, :, :, :].rearrange("p n a d -> p (n a d)")
        b1_all = sb("b1_all", [P, NE * DM])
        pairs = sb("pairs", [2, (NE + 3) * D], fp32r)
        B_IN, B_2, B_OUT, B_C = 0, 1, NE + 1, NE + 2
        rows = sb("rows", [P, TRIO, D])
        made = sb("made", [P, TILES, D])
        back = [sb(f"back{k}", [P, NJ, D]) for k in range(2)]
        midhi, midlo = sb("midhi", [P, TRIO, DM], fp32r), sb("midlo", [P, TRIO, DM], fp32r)
        rowThi, rowTlo = sb("rowThi", [P, TRIO, P], fp32r), sb("rowTlo", [P, TRIO, P], fp32r)
        turned_buf = sb("turned_buf", [P, 4, W])
        xT = turned_buf[:, 0:2, :]
        hT = turned_buf[:, 2:4, :]
        mid = turned_buf[:, 0:TRIO, :]
        araw = rows
        braw = b1_all[0:2, 0:(NE + 3) * D]
        bhi = midhi[0:2, :, :].rearrange("p a k -> p (a k)")[:, 0:(NE + 3) * D]
        work = sb("work", [P, NE * DM + 7 * NJ * NE])
        flat_made = made[:, :, :].rearrange("p t d -> p (t d)")
        aT = work[:, 0:NU * W]
        gate_out = flat_made[:, 0:2 * W].rearrange("p (s w) -> p s w", s=2)
        stage1, stage2 = work[:, 0:NE * DM], flat_made[:, 0:NE * NC * D]

        win, wout, w1T = sb("win", [P, D]), sb("wout", [P, D]), sb("w1T", [P, D])
        wcT = sb("wcT", [P, 2, D])
        w2rep, w2col = sb("w2rep", [P, P]), sb("w2col", [P, 1])
        wg = sb("wg", [P, NE])
        bg_all = sb("bg_all", [P, NE])
        ab1, ab2 = sb("ab1", [P, 1]), sb("ab2", [P, 1])
        row_sel, row_not = sb("row_sel", [2, 1]), sb("row_not", [2, 1])
        ident = sb("ident", [P, P])
        before, ones_bf = sb("before", [P, P], bf16), sb("ones_bf", [P, P], bf16)
        ones2f, ones2 = sb("ones2f", [2, P]), sb("ones2", [2, P], fp32r)
        upto = sb("upto", [P, 2 * P])
        one_col = sb("one_col", [P, 1])
        rev_i, rev = sb("rev_i", [P, NE], i32), sb("rev", [P, NE])
        step_i, step128 = sb("step_i", [P, NJ], i32), sb("step128", [P, NJ])
        tile_i, tile_no = sb("tile_i", [P, TILES], i32), sb("tile_no", [P, TILES])
        stats, mv = sb("stats", [P, NJ, 6]), sb("mv", [P, NJ, 2])
        vare, std, rstd = sb("vare", [P, NJ]), sb("std", [P, NJ]), sb("rstd", [P, NJ])
        SMALL = NJ * NE
        lg, lg2, key, hit1, hit2, ex, tmp = (
            work[:, NE * DM + n * SMALL:NE * DM + (n + 1) * SMALL
                      ].rearrange("p (j e) -> p j e", e=NE) for n in range(7))
        cum, pos, over = (
            flat_made[:, NE * DM + n * SMALL:NE * DM + (n + 1) * SMALL
                      ].rearrange("p (e j) -> p e j", e=NE) for n in range(3))
        best, kbest = sb("best", [P, NJ]), sb("kbest", [P, NJ])
        ssum, rsum, p1, p2 = sb("ssum", [P, NJ]), sb("rsum", [P, NJ]), sb("p1", [P, NJ]), sb("p2", [P, NJ])
        hits = sb("hits", [P, NE, NJ], bf16)
        cnt, ctile, tend, tbase = sb("cnt", [P, NE]), sb("ctile", [P, NE]), sb("tend", [P, NE]), sb("tbase", [P, NE])
        past = flat_made[:, NE * DM + 3 * SMALL:NE * DM + 3 * SMALL + TILES * NE].rearrange(
            "p (t e) -> p t e", e=NE)
        posf = sb("posf", [P, 2, NJ])
        NQ = 2 * HALVES
        RUN = HALVES * TILES
        TRIOS = RUN // TRIO
        owners = sb("owners", [P, TILES])
        w1_at = sb("w1_at", [P, NQ, TILES], i32)
        flat_w1_at = w1_at[:, :, :].rearrange("p q t -> p (q t)")
        slot = sb("slot", [P, NQ, 2, NJ], i32)
        home_of, home_slot = sb("home_of", [P, 2, NJ], i32), sb("home_slot", [P, 2, NJ], i32)
        home_tile = sb("home_tile", [P, 2, NJ], i32)
        homes = sb("homes", [P, TILES], i32)
        gate = sb("gate", [P, NQ, 2, NJ])
        NB = NU // UPB
        tok_score, tok_weight, block_sum, block_cum, rden = (
            work[:, NU * W + n * NJ:NU * W + (n + 1) * NJ] for n in range(5))
        maxima = work[:, NU * W + 5 * NJ:NU * W + 6 * NJ]
        unit_max, big = maxima[:, 0:NU], maxima[:, NU:NU + NB]

        ps = [ctx.enter_context(nc.psum_tensor(f"bank{i}", [P, 512], fp32)) for i in range(8)]

        OUT_BANKS = [(0, 1), (7, 6)]

        x_in_s = [sem(f"x_loaded{c}") for c in range(4)]
        weights_s, b1_s = sem("expert_weights_loaded"), sem("b1_loaded")
        first_s, small_s = sem("first_small_loaded"), sem("small_loaded")
        w2_s = sem("w2_loaded")
        consts = sem("constants_made")
        zeroed = sem("back_zeroed")
        rows_zero = [sem(f"sorted_rows{h}_zeroed") for h in range(HALVES)]
        split_act, split_dve = sem("weights_hi"), sem("weights_lo")
        aw_turned, aw_copied = sem("attention_weights_turned"), sem("attention_weights_copied")
        chain = sem("vector_step")
        var_ready, std_ready = sem("variance_ready"), sem("std_ready")
        src_ready, turned, turned_out = sem("unit_source_ready"), sem("unit_turned"), sem("unit_copied")
        projected = sem("unit_projected")
        h_ready, x_added, tanh_ready = sem("experts_input_ready"), sem("x_updated"), sem("hidden_ready")
        hT_ps, hT_ready, lg_ps = sem("h_turned"), sem("hT_copied"), sem("logits_done")
        lg_read, ex_in, ex_ready = sem("logits_read"), sem("exp_input"), sem("exp_done")
        hits_ready, rank_ps, rank_read = sem("hits_ready"), sem("ranks_done"), sem("ranks_read")
        slots_ready, owners_ready, gates_ready = sem("slots_ready"), sem("owners_ready"), sem("gates_ready")
        taken_up = [sem(f"taken_up{i}") for i in range(NU)]
        gated = sem("rows_times_gate")
        home_made, home_reset = sem("home_constants_made"), sem("home_reset")
        home_step, home_sent, homes_in, went_home = (sem("home_places"), sem("home_sent"), sem("homes_loaded"),
                                                     sem("rows_went_home"))
        scattered = [sem(f"scattered{h}") for h in range(HALVES)]
        rows_in = [sem(f"rows_loaded{k}") for k in range(TRIO)]
        made_out = sem("made_stored")
        row_turned, rowhi_ready, rowlo_ready = sem("tile_turned"), sem("tile_hi"), sem("tile_lo")
        up_done, mid_ready, mid_turned = sem("up_done"), sem("mid_ready"), sem("mid_turned")
        midhi_ready, midlo_ready = sem("mid_hi"), sem("mid_lo")
        down_done, made_ready = sem("down_done"), sem("tile_made")
        gathered = [sem(f"gathered{i}") for i in range(NU)]
        prep_ready = sem("bias_pairs_ready")
        score_ps, score_max, exp_in, weight_ready = (sem("scores_done"), sem("unit_max_taken"),
                                                     sem("token_scores_ready"), sem("token_weights_ready"))
        weighted_ready, num_ps, num_out = sem("weighted_rows_ready"), sem("sums_done"), sem("sums_copied")
        out_ps, out_read = sem("attention_out_done"), sem("attention_out_read")
        gate_ready, att_x = sem("tanh_output"), sem("attention_added")
        rden_ready, scaled = sem("reciprocals_ready"), sem("attention_out_scaled")
        den_ps, den_read = sem("denominators_turned"), sem("denominators_read")
        stored = sem("out_stored")

        block = ctx.enter_context(nc.Block())

        FIRST_PARTS = ((0, NU // 2), (NU // 2, NU))

        def wait_rows_back(eng, q, i):
            if q < 2 * HALVES - 1:
                eng.wait_ge(gathered[i], 16 * 2 * U * (q + 1))
            else:
                eng.wait_ge(taken_up[i], 16 * 2)

        def q_of(ph):
            return ph[1] * HALVES + ph[2]

        def hT_used(eng, m):
            kind, a = middle_kind[m]
            eng.wait_ge(lg_ps if kind == "route" else score_ps, a + 1)

        x_rows = x_in.rearrange("b t d -> (b t) d").rearrange("(j p) d -> p j d", p=P)
        out_rows = out.rearrange("b t d -> (b t) d").rearrange("(j p) d -> p j d", p=P)

        first_loads = ((win[:, :], f_win), (braw[:, B_IN * D:(B_IN + 1) * D], f_bin.partition_broadcast(2)),
                       (wg[:, :], f_wg), (bg_all[:, :], f_bg.partition_broadcast(P)))
        small_loads = ((braw[:, B_2 * D:(B_2 + NE) * D], f_b2.rearrange("e d -> (e d)").partition_broadcast(2)),
                       (braw[:, B_OUT * D:(B_OUT + 1) * D], f_bout.partition_broadcast(2)),
                       (braw[:, B_C * D:(B_C + 1) * D], a_bc.partition_broadcast(2)),
                       (wout[:, :], f_wout),
                       (ab1[:, :], a_b1.rearrange("(p a) -> p a", a=1)),
                       (ab2[:, :], a_b2.partition_broadcast(P)),
                       (w2col[:, :], a_w2.rearrange("a p -> p a")),
                       (araw[:, 0, :], a_w1),
                       (araw[:, 1:3, :], a_wc.rearrange("p (a k) -> p a k", a=2)))

        @block.sync
        def _(sp):
            def load_x(quarters):
                for c in quarters:
                    sp.dma_start(X[:, 8 * c:8 * c + 8, :], x_rows[:, 8 * c:8 * c + 8, :]).then_inc(x_in_s[c], 16)

            load_x((0, 1))
            for dst, src in small_loads:
                sp.dma_start(dst, src).then_inc(small_s, 16)
            load_x((2, 3))
            sp.wait_ge(zeroed, 2)

            def zero_rows(h):
                by_partition = sorted_rows[h].rearrange("(p r) d -> p r d", p=P)
                for k, (r0, n) in enumerate(((0, NJ), (NJ, NJ), (2 * NJ, TILES - 2 * NJ))):
                    sp.dma_start(by_partition[:, r0:r0 + n, :], back[k % 2][:, 0:n, :]).then_inc(rows_zero[h], 16)

            zero_rows(0)
            sp.wait_ge(home_made, 2)
            sp.dma_start(home.rearrange("(p t) a -> p (t a)", p=P), homes[:, :]).then_inc(home_reset, 16)
            sp.dma_start(stage1.rearrange("p (e m) -> p e m", e=NE),
                         f_w1.rearrange("e d m -> d e m")).then_inc(weights_s, 16)
            sp.dma_start(stage2.rearrange("p (e c d) -> p e c d", e=NE, c=NC),
                         f_w2.rearrange("e (c p) d -> p e c d", p=P)).then_inc(w2_s, 16)
            zero_rows(1)
            sp.wait_ge(prep_ready, 2)
            sp.dma_start(b1_all[:, :], f_b1.rearrange("e m -> (e m)").partition_broadcast(P)).then_inc(b1_s, 16)
            for ph in PLAN:
                kind, f, h = ph
                q = q_of(ph)
                if kind == "experts":
                    base = RUN * f
                    if f == 0:
                        sp.wait_ge(aw_turned, 1)
                    kept = HALVES if f == 0 else 1

                    def load(half, i):
                        first = base + half * TILES
                        for k in range(TRIO):
                            if first > 0 or not isinstance(i, int) or i > 0:
                                sp.wait_ge(row_turned, first + TRIO * i + k - TRIO + 1)
                            sp.dma_start(rows[:, k, :], sorted_rows[half][ds((TRIO * i + k) * P, P), :]
                                         ).then_inc(rows_in[k], 16)

                    def store(half, i):
                        if half < kept:
                            sp.wait_ge(made_ready, base + half * TILES + TRIO * i + TRIO)
                            sp.dma_start(expert_out[half][ds(TRIO * i * P, TRIO * P), :].rearrange(
                                "(t p) d -> p t d", p=P), made[:, ds(TRIO * i, TRIO), :]).then_inc(made_out, 16)

                    for half in range(HALVES):
                        sp.wait_ge(scattered[half], 16 * 2 * NJ * (f + 1))
                        for i in range(2):
                            load(half, i)
                            if half:
                                store(half - 1, STORES - 2 + i)
                        with sp.Fori(2, STORES) as trio:
                            load(half, trio)
                            store(half, trio - 2)
                        if f == 1 and half == 0:
                            sp.wait_ge(home_sent, 16 * 2 * NJ)
                            sp.dma_start(homes[:, :], home.rearrange("(p t) a -> p (t a)", p=P)
                                         ).then_inc(homes_in, 16)
                    store(HALVES - 1, STORES - 2)
                    store(HALVES - 1, STORES - 1)
                    if f == 1:
                        sp.wait_ge(went_home, 16 * TILES)
                        for i in range(NU):
                            sp.wait_ge(turned, unit[("combine", 1, 0), i] + 1)
                            for k in range(2):
                                at = (k * NJ + U * i) * P
                                sp.dma_start(back[k][:, U * i:U * i + U, :], rows_home[at:at + U * P, :].rearrange(
                                    "(j p) d -> p j d", p=P)).then_inc(taken_up[i], 16)
                if kind == "combine" and f == 1:
                    for i in range(NU):
                        sp.wait_ge(x_added, kind_unit[ph, i] + 1)
                        j = h * NJ + U * i
                        sp.dma_start(out_rows[:, j:j + U, :], X[:, j:j + U, :]).then_inc(stored, 16)
            sp.wait_ge(stored, 16 * HALVES * NU)

        @block.gpsimd
        def _(pool):
            pool.memset(ident[:, :], 0.0).then_inc(consts, 1)
            pool.memset(before[:, :], 1.0).then_inc(consts, 1)
            pool.memset(ones_bf[:, :], 1.0).then_inc(consts, 1)
            pool.memset(ones2f[:, :], 1.0).then_inc(consts, 1)
            pool.memset(upto[:, :], 1.0).then_inc(consts, 1)
            pool.memset(one_col[:, :], 1.0).then_inc(consts, 1)
            pool.memset(row_sel[:, :], 0.0).then_inc(consts, 1)
            pool.memset(row_not[:, :], 1.0).then_inc(consts, 1)
            pool.wait_ge(consts, 8)
            pool.affine_select(out=ident[:, :], in_=ident[:, :], compare_op=ALU.not_equal, fill=1.0, base=0,
                               pattern=[[-1, P]], channel_multiplier=1).then_inc(consts, 1)
            pool.affine_select(out=before[:, :], in_=before[:, :], compare_op=ALU.is_gt, fill=0.0, base=0,
                               pattern=[[1, P]], channel_multiplier=-1).then_inc(consts, 1)
            pool.affine_select(out=upto[:, 0:P], in_=upto[:, 0:P], compare_op=ALU.is_ge, fill=0.0, base=0,
                               pattern=[[1, P]], channel_multiplier=-1).then_inc(consts, 1)
            pool.affine_select(out=row_sel[:, :], in_=row_sel[:, :], compare_op=ALU.not_equal, fill=1.0, base=0,
                               pattern=[[0, 1]], channel_multiplier=1).then_inc(consts, 1)
            pool.affine_select(out=row_not[:, :], in_=row_not[:, :], compare_op=ALU.not_equal, fill=0.0, base=0,
                               pattern=[[0, 1]], channel_multiplier=1).then_inc(consts, 1)
            pool.memset(back[0][:, :, :], 0.0).then_inc(zeroed, 1)
            pool.memset(back[1][:, :, :], 0.0).then_inc(zeroed, 1)
            pool.iota(home_of[:, :, :], pattern=[[NJ * P, 2], [P, NJ]], base=0, channel_multiplier=1
                      ).then_inc(home_made, 1)
            pool.iota(homes[:, :], pattern=[[P, TILES]], base=2 * NJ * P, channel_multiplier=1
                      ).then_inc(home_made, 1)
            pool.iota(rev_i[:, :], pattern=[[-1, NE]], base=NE, channel_multiplier=0).then_inc(consts, 1)
            pool.iota(step_i[:, :], pattern=[[P, NJ]], base=0, channel_multiplier=0).then_inc(consts, 1)
            pool.iota(tile_i[:, :], pattern=[[1, TILES]], base=0, channel_multiplier=0).then_inc(consts, 1)

            def scatter(f, h):
                q = f * HALVES + h
                if f == 0:
                    pool.wait_ge(rows_zero[h], 16 * 3)
                pool.wait_ge(slots_ready, q + 1)
                pool.wait_ge(h_ready, NU * (q + 1))
                if f == 1:
                    pool.wait_ge(row_turned, TILES * HALVES)
                for j in range(NJ):
                    for k in range(2):
                        pool.indirect_dma_start(
                            sorted_rows[h], bass.IndirectOffsetOnAxis(slot[:, q, k, j:j + 1], 0),
                            H[h][:, j, :], None).then_inc(scattered[h], 16)

            def gather(f, h):
                q = f * HALVES + h
                pool.wait_ge(made_out, 16 * STORES * (q + 1))
                for i in range(NU):
                    if q > 0:
                        last = ("combine", (q - 1) // HALVES, (q - 1) % HALVES)
                        pool.wait_ge(turned, unit[last, i] + 1)
                    for j in range(U * i, U * i + U):
                        for k in range(2):
                            pool.indirect_dma_start(
                                back[k][:, j, :], None, expert_out[h],
                                bass.IndirectOffsetOnAxis(slot[:, q, k, j:j + 1], 0)).then_inc(gathered[i], 16)

            def send_homes(q):
                pool.wait_ge(home_step, 3)
                pool.wait_ge(home_reset, 16)
                for k in range(2):
                    for j in range(NJ):
                        pool.indirect_dma_start(
                            home, bass.IndirectOffsetOnAxis(home_slot[:, k, j:j + 1], 0),
                            home_of[:, k, j:j + 1], None).then_inc(home_sent, 16)

            def go_home(q):
                pool.wait_ge(homes_in, 16)
                for t in range(TILES):
                    pool.wait_ge(made_ready, q * TILES + t + 1)
                    pool.indirect_dma_start(
                        rows_home, bass.IndirectOffsetOnAxis(homes[:, t:t + 1], 0),
                        made[:, t, :], None).then_inc(went_home, 16)

            scatter(0, 0)
            scatter(0, 1)
            gather(0, 0)
            gather(0, 1)
            scatter(1, 0)
            scatter(1, 1)
            send_homes(2 * HALVES - 1)
            gather(1, 0)
            go_home(2 * HALVES - 1)

        @block.scalar
        def _(act):
            for dst, src in first_loads:
                act.dma_start(dst, src).then_inc(first_s, 16)

            def copy_unit(ph, i, dst):
                act.wait_ge(turned, unit[ph, i] + 1)
                act.activation(dst, ps[unit[ph, i] % 2][:, :], ACT.Copy).then_inc(turned_out, 1)

            def xT_of(ph, i):
                n = unit[ph, i]
                if n >= 2:
                    act.wait_ge(projected, n - 1)
                copy_unit(ph, i, xT[:, n % 2, :])

            def root(n, units=(0, NU)):
                of = slice(U * units[0], U * units[1])
                act.wait_ge(var_ready, n + 1)
                act.activation(std[:, of], vare[:, of], ACT.Sqrt).then_inc(std_ready, 1)

            def times_gate(ph, i):
                q = q_of(ph)
                act.wait_ge(gates_ready, q + 1)
                wait_rows_back(act, q, i)
                for j in range(U * i, U * i + U):
                    last = act.activation(back[1][:, j, :], back[1][:, j, :], ACT.Copy,
                                          scale=gate[:, q, 1, j:j + 1])
                last.then_inc(gated, 1)

            def exponents(q):
                act.wait_ge(ex_in, q + 1)
                act.activation(ex[:, :, :], tmp[:, :, :], ACT.Exp).then_inc(ex_ready, 1)

            lns = 0
            for ph in PLAN:
                kind, f, h = ph
                q = q_of(ph)
                if kind == "route":
                    if q != 1:
                        root(lns, FIRST_PARTS[0] if q == 0 else (0, NU))
                        lns += 1
                    for i in range(NU + 2):
                        if i < NU:
                            xT_of(ph, i)
                        if q == 0 and i == FIRST_PARTS[1][0] - 1:
                            root(lns, FIRST_PARTS[1])
                            lns += 1
                        if q == 0 and i == 3:
                            root(lns)
                            lns += 1
                        if ph == ROUTED and i == 3:
                            root(lns)
                            lns += 1
                        if 1 <= i <= NU:
                            n = unit[ph, i - 1]
                            act.wait_ge(projected, n + 1)
                            act.activation(H[h][:, U * (i - 1):U * i, :],
                                           ps[2 + n % 2][:, :].rearrange("p (u d) -> p u d", u=U),
                                           ACT.Copy).then_inc(h_ready, 1)
                        if i >= 2:
                            m = middle[ph, i - 2]
                            act.wait_ge(hT_ps, kind_unit[ph, i - 2] + 1)
                            if m >= 2:
                                hT_used(act, m - 2)
                            act.activation(hT[:, m % 2, :], ps[4 + m % 2][:, :], ACT.Copy).then_inc(hT_ready, 1)
                    if q == 1:
                        act.wait_ge(aw_turned, 1)
                        act.activation(w1T[:, :], ps[7][:, 0:D], ACT.Copy).then_inc(aw_copied, 1)
                        act.activation(wcT[:, :, :], ps[7][:, D:3 * D], ACT.Copy).then_inc(aw_copied, 1)
                        exponents(0)
                        act.wait_ge(weights_s, 16)
                        act.activation(w1hi[:, :], stage1, ACT.Copy).then_inc(split_act, 1)
                        act.wait_ge(w2_s, 16)
                        act.activation(w2[:, :, 0, :], stage2.rearrange("p (n d) -> p n d", d=D), ACT.Copy
                                       ).then_inc(split_act, 1)
                    if q > 0 and ph != ROUTED:
                        exponents(q)
                elif kind == "combine":
                    if ph != COMBINED:
                        times_gate(ph, 0)
                    for i in range(NU):
                        if i + 1 < NU and ph != COMBINED:
                            times_gate(ph, i + 1)
                        xT_of(ph, i)
                elif kind == "attention":
                    if ph != BESIDE:
                        root(lns)
                        lns += 1

                    def hidden(i):
                        n, m, a = unit[ph, i], middle[ph, i], kind_unit[ph, i]
                        act.wait_ge(projected, n + 1)
                        if m >= 2:
                            hT_used(act, m - 2)
                        act.activation(hT[:, m % 2, :], ps[2 + n % 2][:, :], ACT.Tanh,
                                       bias=ab1[:, :]).then_inc(tanh_ready, 1)

                    def copy_sums(i):
                        a = kind_unit[ph, i]
                        act.wait_ge(num_ps, a + 1)
                        if i >= 2:
                            act.wait_ge(out_ps, a - 1)
                        for k in range(U):
                            to, of = xT[:, i % 2, k * P:(k + 1) * P], ps[4 + i % 2][:, k * P:(k + 1) * P]
                            if i % UPB == 0 and k == 0:
                                act.activation(to, of, ACT.Copy).then_inc(num_out, 1)
                            else:
                                before_it = xT[:, i % 2, k * P - 1:k * P] if k else xT[:, (i - 1) % 2, W - 1:W]
                                act.wait_ge(num_out, U * a + k)
                                act.activation(to, of, ACT.Identity, bias=before_it).then_inc(num_out, 1)

                    def outs(i):
                        a = kind_unit[ph, i]
                        act.wait_ge(out_read, a + 1)
                        act.activation(gate_out[:, a % 2, :], gate_out[:, a % 2, :], ACT.Tanh).then_inc(gate_ready, 1)

                    def scale_out(i):
                        a = kind_unit[ph, i]
                        act.wait_ge(out_ps, a + 1)
                        if i >= 2:
                            act.wait_ge(att_x, a - 1)
                        for k in range(U):
                            last = act.activation(gate_out[:, a % 2, k * D:(k + 1) * D],
                                                  ps[OUT_BANKS[i % 2][0]][:, k * D:(k + 1) * D], ACT.Copy,
                                                  scale=rden[:, U * i + k:U * i + k + 1])
                        last.then_inc(scaled, 1)

                    for i in range(NU + 1):
                        if i < NU:
                            copy_unit(ph, i, aT[:, i * W:(i + 1) * W])
                        if i >= 1:
                            hidden(i - 1)
                        if ph == BESIDE and i == 2:
                            exponents(q_of(ROUTED))
                        if ph != BESIDE and i in (2, 3):
                            times_gate(COMBINED, i - 2)
                    act.wait_ge(exp_in, h + 1)
                    for b in range(NB):
                        blocks_of = slice(b * U * UPB, (b + 1) * U * UPB)
                        act.activation(tok_weight[:, blocks_of], tok_score[:, blocks_of], ACT.Exp,
                                       bias=big[:, b:b + 1]).then_inc(weight_ready, 1)
                    copy_sums(0)
                    copy_sums(1)
                    if ph != BESIDE:
                        times_gate(COMBINED, 2)
                        times_gate(COMBINED, 3)
                        act.wait_ge(made_out, 16 * STORES * HALVES)
                    act.wait_ge(rden_ready, h + 1)
                    if h:
                        act.wait_ge(att_x, NU * h)
                    scale_out(0)
                    for i in range(NU):
                        if i + 2 < NU:
                            copy_sums(i + 2)
                        outs(i)
                        if i + 1 < NU:
                            scale_out(i + 1)
                else:
                    base = RUN * f

                    def row_hi(s, k):
                        act.wait_ge(row_turned, base + s + 1)
                        act.activation(rowThi[:, k, :], ps[6][:, 0:P], ACT.Copy).then_inc(rowhi_ready, 1)

                    def mid_hi(s, k):
                        act.wait_ge(mid_turned, base + s + 1)
                        act.activation(midhi[:, k, :], ps[3 + k][:, :], ACT.Relu).then_inc(midhi_ready, 1)

                    def turn(s, k):
                        row_hi(s + 1, (k + 1) % TRIO)
                        mid_hi(s - 1, (k + 2) % TRIO)

                    row_hi(0, 0)
                    row_hi(1, 1)
                    row_hi(2, 2)
                    mid_hi(0, 0)
                    turn(2, 2)
                    with act.Fori(1, RUN // TRIO - 1) as trio:
                        for k in range(TRIO):
                            turn(trio * TRIO + k, k)
                    turn(RUN - 3, 0)
                    turn(RUN - 2, 1)
                    mid_hi(RUN - 2, 1)
                    mid_hi(RUN - 1, 2)

        @block.vector
        def _(dve):
            steps = [0]

            def did(ins):
                steps[0] += 1
                return ins.then_inc(chain, 1)

            def settle():
                dve.wait_ge(chain, steps[0])

            def over_e(ap):
                return ap.unsqueeze(2).to_broadcast([P, NJ, NE])

            def over_j(ap):
                return ap.unsqueeze(2).to_broadcast([P, NE, NJ])

            def blocks(ap):
                return ap.rearrange("p (u d) -> p u d", u=U)

            b1_at = [dve.alloc_register(f"b1_at{k}") for k in range(TRIO)]
            dve.wait_ge(consts, 13)
            did(dve.tensor_copy(ones2[:, :], ones2f[:, :]))

            def prepare_biases(first, last):
                raw, hi = braw[:, first * D:last * D], bhi[:, first * D:last * D]
                did(dve.tensor_copy(hi, raw))
                settle()
                did(dve.tensor_tensor(raw, raw, hi.bitcast(fp32), ALU.subtract))
                settle()
                did(dve.tensor_scalar(raw, raw, row_not[:, :], None, ALU.mult))
                settle()
                dve.scalar_tensor_tensor(pairs[:, first * D:last * D], hi.bitcast(fp32), row_sel[:, :], raw,
                                         ALU.mult, ALU.add).then_inc(prep_ready, 1)

            def unit_stats(h, i):
                for j in range(U * i, U * i + U):
                    did(dve.bn_stats(stats[:, j, :], X[:, h * NJ + j, :]))
                settle()
                for j in range(U * i, U * i + U):
                    did(dve.bn_aggr(mv[:, j, :], stats[:, j, :]))

            def layernorm(ph):
                kind, f, h = ph
                for first, end in FIRST_PARTS if layernorm.count == 0 else ((0, NU),):
                    layernorm_part(ph, first, end)

            def layernorm_part(ph, first, end):
                kind, f, h = ph
                j0 = h * NJ
                of = slice(U * first, U * end)
                n = layernorm.count
                layernorm.count += 1
                if kind == "route" and f == 0:
                    for i in range(first, end):
                        if i % 2 == 0:
                            dve.wait_ge(x_in_s[2 * h + i // 2], 16)
                        unit_stats(h, i)
                settle()
                dve.tensor_scalar(vare[:, of], mv[:, of, 1], EPS, None, ALU.add).then_inc(var_ready, 1)
                if n == 0:
                    dve.wait_ge(first_s, 16 * len(first_loads))
                    prepare_biases(B_IN, B_IN + 1)
                dve.wait_ge(std_ready, n + 1)
                did(dve.reciprocal(rstd[:, of], std[:, of]))
                settle()
                if kind == "attention":
                    dve.wait_ge(scattered[h], 16 * 2 * NJ)
                if kind == "route" and f == 1:
                    att = ("attention", 0, h)
                    dve.wait_ge(turned, unit[att, NU - 1] + 1)
                for i in range(first, end):
                    for j in range(U * i, U * i + U):
                        last = dve.tensor_scalar(H[h][:, j, :], X[:, j0 + j, :], mv[:, j, 0:1],
                                                 rstd[:, j:j + 1], ALU.subtract, ALU.mult)
                    last.then_inc(src_ready, 1)

            layernorm.count = 0

            def first_hit(values, hit):
                did(dve.tensor_reduce(best[:, :], values[:, :, :], AX, ALU.max))
                settle()
                did(dve.tensor_tensor(hit[:, :, :], values[:, :, :], over_e(best[:, :]), ALU.is_equal))
                settle()
                did(dve.tensor_tensor(key[:, :, :], hit[:, :, :], rev[:, :].unsqueeze(1).to_broadcast([P, NJ, NE]),
                                      ALU.mult))
                settle()
                did(dve.tensor_reduce(kbest[:, :], key[:, :, :], AX, ALU.max))
                settle()
                did(dve.tensor_tensor(hit[:, :, :], key[:, :, :], over_e(kbest[:, :]), ALU.is_equal))

            def weigh(ph, i):
                q = q_of(ph)
                wait_rows_back(dve, q, i)
                dve.wait_ge(gated, NU * q + i + 1)
                for j in range(U * i, U * i + U):
                    last = dve.scalar_tensor_tensor(back[0][:, j, :], back[0][:, j, :],
                                                    gate[:, q, 0, j:j + 1], back[1][:, j, :],
                                                    ALU.mult, ALU.add)
                last.then_inc(src_ready, 1)

            def add_out(ph, i, with_stats=True):
                kind, f, h = ph
                n = unit[ph, i]
                dve.wait_ge(projected, n + 1)
                Xu = X[:, h * NJ + U * i:h * NJ + U * i + U, :]
                dve.scalar_tensor_tensor(Xu, blocks(ps[2 + n % 2][:, :]), 0.5, Xu,
                                         ALU.mult, ALU.add).then_inc(x_added, 1)
                if f == 0 and with_stats:
                    dve.wait_ge(x_added, kind_unit[ph, i] + 1)
                    unit_stats(h, i)

            def largest_score(ph, i):
                dve.wait_ge(score_ps, kind_unit[ph, i] + 1)
                dve.tensor_reduce(unit_max[:, i:i + 1], ps[4 + middle[ph, i] % 2][:, :], AX, ALU.max
                                  ).then_inc(score_max, 1)

            def choose_experts(q):
                dve.wait_ge(lg_ps, NU * (q + 1))
                dve.tensor_tensor(lg[:, :, :], ps[6][:, 0:NJ * NE].rearrange("p (j e) -> p j e", e=NE),
                                  bg_all[:, :].unsqueeze(1).to_broadcast([P, NJ, NE]), ALU.add
                                  ).then_inc(lg_read, 1)
                dve.wait_ge(lg_read, q + 1)
                first_hit(lg, hit1)
                dve.tensor_tensor(tmp[:, :, :], lg[:, :, :], over_e(best[:, :]), ALU.subtract).then_inc(ex_in, 1)
                settle()
                did(dve.scalar_tensor_tensor(lg2[:, :, :], hit1[:, :, :], -3.0e38, lg[:, :, :],
                                             ALU.mult, ALU.add))
                settle()
                dve.wait_ge(ex_in, q + 1)
                first_hit(lg2, hit2)
                settle()
                dve.tensor_tensor(hits[:, :, :].rearrange("p e j -> p j e"), hit1[:, :, :], hit2[:, :, :],
                                  ALU.add).then_inc(hits_ready, 1)

            def weigh_experts(q):
                dve.wait_ge(ex_ready, q + 1)
                did(dve.tensor_reduce(ssum[:, :], ex[:, :, :], AX, ALU.add))
                did(dve.tensor_tensor(tmp[:, :, :], ex[:, :, :], hit1[:, :, :], ALU.mult))
                did(dve.tensor_tensor(key[:, :, :], ex[:, :, :], hit2[:, :, :], ALU.mult))
                settle()
                did(dve.reciprocal(rsum[:, :], ssum[:, :]))
                did(dve.tensor_reduce(p1[:, :], tmp[:, :, :], AX, ALU.add))
                did(dve.tensor_reduce(p2[:, :], key[:, :, :], AX, ALU.add))
                settle()
                did(dve.tensor_tensor(p1[:, :], p1[:, :], rsum[:, :], ALU.mult))
                did(dve.tensor_tensor(p2[:, :], p2[:, :], rsum[:, :], ALU.mult))
                settle()
                did(dve.tensor_tensor(ssum[:, :], p1[:, :], p2[:, :], ALU.add))
                settle()
                did(dve.reciprocal(rsum[:, :], ssum[:, :]))
                settle()
                did(dve.tensor_tensor(gate[:, q, 0, :], p1[:, :], rsum[:, :], ALU.mult))
                dve.tensor_tensor(gate[:, q, 1, :], p2[:, :], rsum[:, :], ALU.mult).then_inc(gates_ready, 1)

            def place_rows(q, owning):
                dve.wait_ge(rank_ps, q + 1)
                in_block = ps[6][:, 2 * P:3 * P].rearrange("p (e j) -> p e j", e=NE)
                did(dve.tensor_reduce(cnt[:, :], in_block, AX, ALU.add))
                did(dve.tensor_tensor_scan(cum[:, :, :].rearrange("p e j -> p (e j)"),
                                           one_col[:, 0:1].to_broadcast([P, NE * NJ]),
                                           ps[6][:, 2 * P:3 * P], 0.0, ALU.mult, ALU.add))
                settle()
                did(dve.tensor_tensor(over[:, :, :], over_j(cnt[:, :]),
                                      step128[:, :].unsqueeze(1).to_broadcast([P, NE, NJ]), ALU.is_gt))
                did(dve.tensor_tensor(cum[:, :, :], cum[:, :, :], in_block, ALU.subtract))
                settle()
                did(dve.tensor_reduce(ctile[:, :], over[:, :, :], AX, ALU.add))
                dve.tensor_tensor(pos[:, :, :], ps[6][:, P:2 * P].rearrange("p (e j) -> p e j", e=NE),
                                  cum[:, :, :], ALU.add).then_inc(rank_read, 1)
                settle()
                did(dve.tensor_tensor_scan(tend[:, :], one_col[:, 0:1].to_broadcast([P, NE]), ctile[:, :], 0.0,
                                           ALU.mult, ALU.add))
                did(dve.scalar_tensor_tensor(tbase[:, :], ctile[:, :], float(P), cum[:, :, 0],
                                             ALU.mult, ALU.add))
                settle()
                did(dve.scalar_tensor_tensor(tbase[:, :], tend[:, :], float(P), tbase[:, :],
                                             ALU.mult, ALU.subtract))
                if owning:
                    own_step(q, 0)
                settle()
                dve.wait_ge(rank_read, q + 1)
                did(dve.tensor_tensor(pos[:, :, :], pos[:, :, :], over_j(tbase[:, :]), ALU.add))
                if owning:
                    own_step(q, 1)
                settle()
                places = pos[:, :, :].rearrange("p e j -> p j e")
                did(dve.tensor_tensor(key[:, :, :], hit1[:, :, :], places, ALU.mult))
                did(dve.tensor_tensor(lg2[:, :, :], hit2[:, :, :], places, ALU.mult))
                if owning:
                    own_step(q, 2)
                settle()
                did(dve.tensor_reduce(posf[:, 0, :], key[:, :, :], AX, ALU.add))
                did(dve.tensor_reduce(posf[:, 1, :], lg2[:, :, :], AX, ALU.add))
                if owning:
                    own_step(q, 3)
                settle()
                dve.tensor_copy(slot[:, q, :, :], posf[:, :, :]).then_inc(slots_ready, 1)

            def place_homes(q):
                dve.wait_ge(slots_ready, q + 1)
                dve.tensor_scalar(home_tile[:, :, :], slot[:, q, :, :], 7, None, ALU.arith_shift_right
                                  ).then_inc(home_step, 1)
                dve.tensor_scalar(home_slot[:, :, :], slot[:, q, :, :], P - 1, None, ALU.bitwise_and
                                  ).then_inc(home_step, 1)
                dve.wait_ge(home_step, 2)
                dve.scalar_tensor_tensor(home_slot[:, :, :], home_slot[:, :, :], float(TILES),
                                         home_tile[:, :, :], ALU.mult, ALU.add).then_inc(home_step, 1)

            def own_step(q, step):
                if step == 0:
                    did(dve.tensor_tensor(past[:, :, :], tile_no[:, :].unsqueeze(2).to_broadcast([P, TILES, NE]),
                                          tend[:, :].unsqueeze(1).to_broadcast([P, TILES, NE]), ALU.is_ge))
                elif step == 1:
                    did(dve.tensor_reduce(owners[:, :], past[:, :, :], AX, ALU.add))
                elif step == 2:
                    did(dve.tensor_scalar(owners[:, :], owners[:, :], float(NE - 1), float(DM), ALU.min, ALU.mult))
                else:
                    dve.tensor_copy(w1_at[:, q, :], owners[:, :]).then_inc(owners_ready, 1)

            def own_tiles(q):
                for step in range(4):
                    own_step(q, step)
                    settle()
                dve.wait_ge(owners_ready, q + 1)

            for ph in PLAN:
                kind, f, h = ph
                q = q_of(ph)
                if kind == "route":
                    if q == 0:
                        layernorm(ph)
                        layernorm(("route", 0, 1))
                        dve.wait_ge(consts, 16)
                        did(dve.tensor_copy(rev[:, :], rev_i[:, :]))
                        did(dve.tensor_copy(step128[:, :], step_i[:, :]))
                        did(dve.tensor_copy(tile_no[:, :], tile_i[:, :]))
                    if q == 2 * HALVES - 1:
                        own_tiles(q_of(ROUTED))
                        weigh_experts(q_of(ROUTED))
                    choose_experts(q)
                    if ph == ROUTED:
                        largest_score(BESIDE, 0)
                        largest_score(BESIDE, 1)
                    place_rows(q, owning=h == 1)
                    if h == 1:
                        dve.wait_ge(owners_ready, q + 1)
                    elif ph != ROUTED:
                        own_tiles(q)
                    if q == 0:
                        dve.wait_ge(small_s, 16 * len(small_loads))
                        prepare_biases(B_2, B_C + 1)
                        did(dve.tensor_copy(w2rep[:, :], w2col[:, 0:1].to_broadcast([P, P])))
                        weigh_experts(q)
                    if q == 1:
                        dve.wait_ge(split_act, 2)
                        dve.tensor_tensor(w1lo[:, :], stage1, w1hi[:, :].bitcast(fp32),
                                          ALU.subtract).then_inc(split_dve, 1)
                        dve.tensor_tensor(w2[:, :, 1, :], stage2.rearrange("p (n d) -> p n d", d=D),
                                          w2[:, :, 0, :].bitcast(fp32), ALU.subtract).then_inc(split_dve, 1)
                        dve.wait_ge(b1_s, 16)
                        weigh_experts(q)
                elif kind == "experts":
                    base = RUN * f

                    seen = {m: dve.alloc_register(f"seen{m + 1}_{f}") for m in range(-1, TRIO + 2)}

                    def count(s, m):
                        return seen[s[1] + m] if isinstance(s, tuple) else base + s + m

                    def row_lo(s, k):
                        dve.wait_ge(rowhi_ready, count(s, 2))
                        dve.tensor_tensor(rowTlo[:, k, :], ps[6][:, 0:P], rowThi[:, k, :].bitcast(fp32),
                                          ALU.subtract).then_inc(rowlo_ready, 1)

                    def add_b1(s, k, at):
                        dve.wait_ge(up_done, count(s, 1))
                        dve.tensor_tensor(mid[:, k, :], ps[k][:, :], b1_all[:, ds(at, DM)],
                                          ALU.add).then_inc(mid_ready, 1)

                    def mid_lo(s, k):
                        dve.wait_ge(midhi_ready, count(s, 0))
                        dve.scalar_tensor_tensor(midlo[:, k, :], ps[3 + k][:, :], 0.0,
                                                 midhi[:, k, :].bitcast(fp32), ALU.max,
                                                 ALU.subtract).then_inc(midlo_ready, 1)

                    def take_down(s, k, slot):
                        dve.wait_ge(down_done, count(s, -1))
                        dve.tensor_reduce(flat_made[:, ds(slot * D, D)],
                                          ps[7][:, 0:2 * D].rearrange("p (a d) -> p d a", a=2),
                                          AX, ALU.add).then_inc(made_ready, 1)

                    def fetch(trio):
                        dve.reg_load(b1_at, flat_w1_at[0:1, ds(base + trio * TRIO, TRIO)])

                    def turn(s, k, at, slot, next_trio=None):
                        row_lo(s, (k + 1) % TRIO)
                        add_b1(s, k, at)
                        if next_trio is not None:
                            fetch(next_trio)
                        mid_lo(s, (k + 2) % TRIO)
                        take_down(s, (k + 1) % TRIO, slot - 2)

                    def places():
                        return [dve.snap(b1_at[k], min_val=0, max_val=(NE - 1) * DM) for k in range(TRIO)]

                    row_lo(-1, 0)
                    if f == 1:
                        place_homes(2 * HALVES - 1)
                    row_lo(0, 1)
                    fetch(0)
                    at = places()
                    add_b1(0, 0, at[0])
                    row_lo(1, 2)
                    add_b1(1, 1, at[1])
                    mid_lo(1, 0)
                    stored_before = STORES * HALVES * f
                    if f:
                        dve.wait_ge(made_out, 16 * stored_before)
                    turn(2, 2, at[2], 2)
                    fetch(1)

                    def loop(first, end, left):
                        for m in seen:
                            dve.reg_mov(seen[m], base + TRIO * first + m)
                        with dve.Fori(first, end) as trio:
                            at = places()
                            for k in range(TRIO):
                                turn(("loop", k), k, at[k], trio * TRIO + k - left,
                                     trio + 1 if k == TRIO - 1 else None)
                            for m in seen:
                                dve.reg_add(seen[m], seen[m], TRIO)

                    loop(1, STORES, 0)
                    at = places()
                    turn(TILES, 0, at[0], TILES)
                    turn(TILES + 1, 1, at[1], TILES + 1)
                    dve.wait_ge(made_out, 16 * (stored_before + STORES - 2))
                    turn(TILES + 2, 2, at[2], 2, STORES + 1)
                    dve.wait_ge(made_out, 16 * (stored_before + STORES))
                    loop(STORES + 1, TRIOS - 1, TILES)
                    at = places()
                    turn(RUN - 3, 0, at[0], TILES - 3)
                    turn(RUN - 2, 1, at[1], TILES - 2)
                    add_b1(RUN - 1, 2, at[2])
                    mid_lo(RUN - 1, 1)
                    take_down(RUN - 1, 0, TILES - 3)
                    mid_lo(RUN, 2)
                    take_down(RUN, 1, TILES - 2)
                    weigh(("combine", f, 0), 0)
                    take_down(RUN + 1, 2, TILES - 1)
                    for m in seen:
                        dve.free_register(seen[m])
                elif kind == "combine":
                    if ph != COMBINED:
                        if h == 1:
                            weigh(ph, 0)
                        weigh(ph, 1)
                        if f == 1 and h == 0:
                            weigh_experts(2 * HALVES - 1)
                        for i in range(NU):
                            if i + 2 < NU:
                                weigh(ph, i + 2)
                            add_out(ph, i)
                else:
                    if ph != BESIDE:
                        layernorm(ph)
                    for i in range(NU):
                        if ph != BESIDE or i >= 2:
                            largest_score(ph, i)
                        if ph != BESIDE and i in (1, 2):
                            weigh(COMBINED, i - 1)
                    did(dve.tensor_scalar(tok_score[:, :], ps[7][:, 0:NJ], ab2[:, :], None, ALU.add))
                    dve.wait_ge(score_max, NU * (h + 1))
                    did(dve.tensor_reduce(big[:, :], unit_max[:, :].rearrange("p (b i) -> p b i", b=NB), AX, ALU.max))
                    settle()
                    dve.tensor_scalar(big[:, :], big[:, :], ab2[:, :], -1.0, ALU.add, ALU.mult).then_inc(exp_in, 1)
                    dve.wait_ge(turned, unit[ph, NU - 1] + 1)
                    dve.wait_ge(weight_ready, NB * (h + 1))
                    def weigh_rows(i):
                        for j in range(U * i, U * i + U):
                            last = dve.tensor_scalar(H[h][:, j, :], H[h][:, j, :], tok_weight[:, j:j + 1], None,
                                                     ALU.mult)
                        last.then_inc(weighted_ready, 1)

                    weigh_rows(0)
                    weigh_rows(1)
                    dve.wait_ge(den_ps, h + 1)
                    did(dve.tensor_copy(block_sum[:, :], ps[7][:, NJ:2 * NJ]))
                    settle()
                    for b in range(NB):
                        bs = slice(b * U * UPB, (b + 1) * U * UPB)
                        did(dve.tensor_tensor_scan(block_cum[:, bs], one_col[:, 0:1].to_broadcast([P, U * UPB]),
                                                   block_sum[:, bs], 0.0, ALU.mult, ALU.add))
                    settle()
                    did(dve.tensor_tensor(block_cum[:, :], block_cum[:, :], block_sum[:, :], ALU.subtract))
                    settle()
                    dve.tensor_tensor(block_cum[:, :], block_cum[:, :], ps[7][:, 0:NJ], ALU.add).then_inc(den_read, 1)
                    weigh_rows(2)
                    weigh_rows(3)
                    dve.wait_ge(den_read, h + 1)
                    dve.reciprocal(rden[:, :], block_cum[:, :]).then_inc(rden_ready, 1)
                    if ph != BESIDE:
                        weigh(COMBINED, 2)
                        weigh(COMBINED, 3)

                    def pre(i):
                        a = kind_unit[ph, i]
                        g = gate_out[:, a % 2, :]
                        dve.wait_ge(scaled, a + 1)
                        dve.tensor_tensor(g, ps[OUT_BANKS[i % 2][1]][:, :], g, ALU.add).then_inc(out_read, 1)

                    def add_att(i):
                        a = kind_unit[ph, i]
                        dve.wait_ge(gate_ready, a + 1)
                        Xu = X[:, h * NJ + U * i:h * NJ + U * i + U, :]
                        dve.tensor_tensor(Xu, Xu, blocks(gate_out[:, a % 2, :]), ALU.add).then_inc(att_x, 1)
                        dve.wait_ge(att_x, a + 1)
                        unit_stats(h, i)

                    pre(0)
                    for i in range(1, NU):
                        pre(i)
                        add_att(i - 1)
                    if ph != BESIDE:
                        add_out(COMBINED, 0, with_stats=False)
                    add_att(NU - 1)
                    if ph != BESIDE:
                        add_out(COMBINED, 1, with_stats=False)
                    layernorm(("route", 1, h))
                    if ph != BESIDE:
                        add_out(COMBINED, 2, with_stats=False)
                        add_out(COMBINED, 3, with_stats=False)
                        dve.wait_ge(x_added, kind_unit[COMBINED, NU - 1] + 1)
                        for i in range(NU):
                            unit_stats(1, i)
                        layernorm(BESIDE)

        @block.tensor
        def _(pe):
            def bank_free(n):
                kind, a = unit_kind[n]
                pe.wait_ge({"route": h_ready, "combine": x_added, "attention": tanh_ready}[kind], a + 1)

            def middle_free(m):
                kind, a = middle_kind[m]
                pe.wait_ge(hT_ready if kind == "route" else score_max, a + 1)

            def transpose_unit(ph, i, src):
                n = unit[ph, i]
                pe.wait_ge(src_ready, n + 1)
                if n >= 2:
                    pe.wait_ge(turned_out, n - 1)
                for k in range(U):
                    last = pe.transpose(ps[n % 2][:, k * P:(k + 1) * P], src[:, U * i + k, :], ident[:, :])
                last.then_inc(turned, 1)

            def bias_row(bank, which):
                pe.matmul(bank[:, :], ones2[:, :], pairs[:, which * D:(which + 1) * D].unsqueeze(1)
                          .to_broadcast([2, U, D]), start=True, stop=False)

            def project(ph, i, weights, which):
                pe.wait_ge(prep_ready, 1 if which == B_IN else 2)
                n = unit[ph, i]
                pe.wait_ge(turned_out, n + 1)
                if n >= 2:
                    bank_free(n - 2)
                bias_row(ps[2 + n % 2], which)
                for k in range(U):
                    last = pe.matmul(ps[2 + n % 2][:, k * D:(k + 1) * D], xT[:, n % 2, k * P:(k + 1) * P],
                                     weights[:, :], start=False, stop=k == U - 1)
                last.then_inc(projected, 1)

            def ranks(q):
                pe.wait_ge(hits_ready, q + 1)
                if q > 0:
                    pe.wait_ge(rank_read, q)
                flat_hits = hits[:, :, :].rearrange("p e j -> p (e j)")
                pe.matmul(ps[6][:, P:2 * P], before[:, :], flat_hits, start=True, stop=True)
                pe.matmul(ps[6][:, 2 * P:3 * P], ones_bf[:, :], flat_hits, start=True, stop=True
                          ).then_inc(rank_ps, 1)

            up_at = [pe.alloc_register(f"up_at{k}") for k in range(TRIO)]
            down_at = [pe.alloc_register(f"down_at{k}") for k in range(TRIO)]

            def keep_warm(products):
                for _ in range(products):
                    pe.transpose(ps[7][:, 0:P], ident[:, :], ident[:, :])

            pe.wait_ge(consts, 13)
            pe.wait_ge(first_s, 16 * len(first_loads))

            for ph in PLAN:
                kind, f, h = ph
                q = q_of(ph)
                if kind == "route":
                    if f == 1:
                        pe.wait_ge(out_read, NU * (h + 1))
                        keep_warm(16)
                    for i in range(NU + 3):
                        if i < NU:
                            transpose_unit(ph, i, H[h])
                        if 1 <= i <= NU:
                            project(ph, i - 1, win, B_IN)
                        if 2 <= i <= NU + 1:
                            m = middle[ph, i - 2]
                            pe.wait_ge(h_ready, kind_unit[ph, i - 2] + 1)
                            if m >= 2:
                                middle_free(m - 2)
                            for k in range(U):
                                last = pe.transpose(ps[4 + m % 2][:, k * P:(k + 1) * P],
                                                    H[h][:, U * (i - 2) + k, :], ident[:, :])
                            last.then_inc(hT_ps, 1)
                        if i >= 3:
                            m = middle[ph, i - 3]
                            pe.wait_ge(hT_ready, kind_unit[ph, i - 3] + 1)
                            if i == 3 and q > 0:
                                pe.wait_ge(rank_read, q)
                            for k in range(U):
                                at = (U * (i - 3) + k) * NE
                                last = pe.matmul(ps[6][:, at:at + NE], hT[:, m % 2, k * P:(k + 1) * P],
                                                 wg[:, :], start=True, stop=True)
                            last.then_inc(lg_ps, 1)
                        if q == 1 and i == 1:
                            ranks(0)
                    if q == 1:
                        pe.wait_ge(small_s, 16 * len(small_loads))
                        for k in range(3):
                            last = pe.transpose(ps[7][:, k * P:(k + 1) * P], araw[:, k, :], ident[:, :])
                        last.then_inc(aw_turned, 1)
                    if q > 0 and ph != ROUTED:
                        ranks(q)
                    if q == 2 * HALVES - 1:
                        keep_warm(22)
                elif kind == "combine":
                    if h == 0:
                        pe.wait_ge(mid_ready, RUN * (f + 1))
                        pe.wait_ge(midlo_ready, RUN * (f + 1))
                    if ph == COMBINED:
                        pe.wait_ge(out_read, NU - 1)
                    for i in range(NU + 1):
                        if i < NU:
                            transpose_unit(ph, i, back[0])
                        if h == 0 and i == 0:
                            pe.wait_ge(made_ready, RUN * (f + 1))
                        if i >= 1:
                            project(ph, i - 1, wout, B_OUT)
                elif kind == "attention":
                    for i in range(NU + 2):
                        if i < NU:
                            transpose_unit(ph, i, H[h])
                        if 1 <= i <= NU:
                            n = unit[ph, i - 1]
                            pe.wait_ge(turned_out, n + 1)
                            bank_free(n - 2)
                            pe.matmul(ps[2 + n % 2][:, :], w1T[:, :], aT[:, (i - 1) * W:i * W],
                                      start=True, stop=True).then_inc(projected, 1)
                        if i >= 2:
                            m, a = middle[ph, i - 2], kind_unit[ph, i - 2]
                            pe.wait_ge(tanh_ready, a + 1)
                            middle_free(m - 2)
                            pe.matmul(ps[4 + m % 2][:, :], w2rep[:, :], hT[:, m % 2, :],
                                      start=True, stop=True)
                            if i == 2:
                                if h:
                                    pe.wait_ge(out_read, NU * h)
                            for k in range(U):
                                at = U * (i - 2) + k
                                last = pe.matmul(ps[7][:, at:at + 1], hT[:, m % 2, k * P:(k + 1) * P], w2col[:, :],
                                                 start=True, stop=True)
                            last.then_inc(score_ps, 1)
                        if ph == BESIDE and i == 2:
                            ranks(q_of(ROUTED))
                    def out_x(i):
                        if i == 1:
                            pe.wait_ge(rank_read, HALVES + h)
                        of_x = ps[OUT_BANKS[i % 2][1]]
                        bias_row(of_x, B_C)
                        for k in range(U):
                            pe.matmul(of_x[:, k * D:(k + 1) * D], aT[:, i * W + k * P:i * W + (k + 1) * P],
                                      wcT[:, 1, :], start=False, stop=k == U - 1)

                    pe.wait_ge(turned_out, unit[ph, NU - 1] + 1)
                    out_x(0)
                    out_x(1)
                    pe.wait_ge(weight_ready, NB * (h + 1))
                    pe.matmul(ps[7][:, 0:NJ], upto[:, 0:P], tok_weight[:, :], start=True, stop=True)
                    pe.matmul(ps[7][:, NJ:2 * NJ], upto[:, P:2 * P], tok_weight[:, :], start=True, stop=True
                              ).then_inc(den_ps, 1)
                    pe.wait_ge(score_max, NU * (h + 1))

                    def sums(i):
                        bank = ps[4 + i % 2]
                        pe.wait_ge(weighted_ready, NU * h + i + 1)
                        if i >= 2:
                            pe.wait_ge(num_out, U * (kind_unit[ph, i] - 1))
                        for k in range(U):
                            last = pe.matmul(bank[:, k * P:(k + 1) * P], H[h][:, U * i + k, :], upto[:, 0:P],
                                             start=True, stop=True)
                        last.then_inc(num_ps, 1)

                    def outs(i):
                        a = kind_unit[ph, i]
                        pe.wait_ge(num_out, U * (a + 1))
                        if i >= 2:
                            pe.wait_ge(out_read, a - 1)
                            out_x(i)
                        if i == 1:
                            pe.wait_ge(den_read, h + 1)
                        of_sums = ps[OUT_BANKS[i % 2][0]]
                        for k in range(U):
                            last = pe.matmul(of_sums[:, k * D:(k + 1) * D], xT[:, i % 2, k * P:(k + 1) * P],
                                             wcT[:, 0, :], start=True, stop=True)
                        last.then_inc(out_ps, 1)

                    sums(0)
                    sums(1)
                    for i in range(NU):
                        outs(i)
                        if i + 2 < NU:
                            sums(i + 2)
                    pe.wait_ge(out_read, NU * (h + 1))
                else:
                    base = RUN * f
                    last_unit = unit[("route", f, HALVES - 1), NU - 1]
                    pe.wait_ge(turned_out, last_unit + 1)
                    pe.wait_ge(h_ready, NU * HALVES * (f + 1))
                    pe.wait_ge(hT_ready, NU * HALVES * (f + 1))
                    pe.wait_ge(rank_read, HALVES * (f + 1))
                    pe.wait_ge(aw_copied, 2)

                    seen = {m: pe.alloc_register(f"seen{m + 2}_{f}") for m in range(-2, TRIO + 2)}
                    loads_seen = pe.alloc_register(f"loads_seen_{f}")

                    def count(s, m):
                        return seen[s[1] + m] if isinstance(s, tuple) else base + s + m

                    def turn_row(loads, k):
                        pe.wait_ge(rows_in[k], loads)
                        pe.transpose(ps[6][:, 0:P], rows[:, k, :], ident[:, :]).then_inc(row_turned, 1)

                    def up(k, at):
                        pe.matmul(ps[k][:, :], rowThi[:, k, :], w1hi[:, ds(at, DM)], start=True, stop=False)
                        pe.matmul(ps[k][:, :], rowThi[:, k, :], w1lo[:, ds(at, DM)], start=False, stop=False)
                        pe.matmul(ps[k][:, :], rowTlo[:, k, :], w1hi[:, ds(at, DM)], start=False, stop=True
                                  ).then_inc(up_done, 1)

                    def turn_mid(s, k):
                        pe.wait_ge(mid_ready, count(s, 0))
                        for c in range(NC):
                            last = pe.transpose(ps[3 + k][:, c * P:(c + 1) * P], mid[:, k, c * P:(c + 1) * P],
                                                ident[:, :])
                        last.then_inc(mid_turned, 1)

                    def down(s, k, at):
                        pe.wait_ge(midlo_ready, count(s, -1))
                        if f > 0 or not s == 2:
                            pe.wait_ge(made_ready, count(s, -2))
                        both, first = ps[7][:, 0:2 * D], ps[7][:, 0:D]
                        for c in range(NC):
                            chunk = flat_w2[:, c * 2 * D:]
                            pe.matmul(both, midhi[:, k, c * P:(c + 1) * P], chunk[:, ds(at * 2, 2 * D)],
                                      start=c == 0, stop=False)
                            pe.matmul(first, midlo[:, k, c * P:(c + 1) * P], chunk[:, ds(at * 2, D)],
                                      start=False, stop=False)
                        pe.matmul(first, ones2[:, :], b2_of(at), start=False, stop=True).then_inc(down_done, 1)

                    def b2_of(at):
                        return pairs[:, B_2 * D:][:, ds(at // (DM // D), D)]

                    def row_and_up(s, k, at, loads):
                        pe.wait_ge(rowlo_ready, count(s, 1))
                        turn_row(loads, (k + 1) % TRIO)
                        up(k, at)

                    def fetch(trio):
                        pe.reg_load(up_at, flat_w1_at[0:1, ds(base + trio * TRIO, TRIO)])

                    def keep():
                        for k in range(TRIO):
                            pe.reg_mov(down_at[k], up_at[k])

                    def places(registers):
                        return [pe.snap(reg, min_val=0, max_val=(NE - 1) * DM) for reg in registers]

                    first_load = 16 * (TRIOS * f + 1)
                    turn_row(first_load, 0)
                    pe.wait_ge(split_dve, 2)
                    pe.wait_ge(owners_ready, HALVES * (f + 1))
                    fetch(0)
                    at = places(up_at)
                    row_and_up(0, 0, at[0], first_load)
                    row_and_up(1, 1, at[1], first_load)
                    turn_mid(1, 0)
                    row_and_up(2, 2, at[2], first_load + 16)
                    keep()
                    fetch(1)
                    for m in seen:
                        pe.reg_mov(seen[m], base + TRIO + m)
                    pe.reg_mov(loads_seen, first_load + 16)
                    turn_mid(2, 1)
                    down(2, 0, at[0])
                    row_and_up(3, 0, places(up_at)[0], first_load + 16)
                    with pe.Fori(1, TRIOS - 1) as trio:
                        at, before_at = places(up_at), places(down_at[1:])
                        turn_mid(("loop", 0), 2)
                        down(("loop", 0), 1, before_at[0])
                        row_and_up(("loop", 1), 1, at[1], loads_seen)
                        turn_mid(("loop", 1), 0)
                        down(("loop", 1), 2, before_at[1])
                        pe.reg_add(loads_seen, loads_seen, 16)
                        row_and_up(("loop", 2), 2, at[2], loads_seen)
                        keep()
                        fetch(trio + 1)
                        turn_mid(("loop", 2), 1)
                        down(("loop", 2), 0, at[0])
                        row_and_up(("loop", 3), 0, places(up_at)[0], loads_seen)
                        for m in seen:
                            pe.reg_add(seen[m], seen[m], TRIO)
                    at, before_at = places(up_at), places(down_at[1:])
                    last_load = first_load + 16 * (TRIOS - 1)
                    turn_mid(RUN - 3, 2)
                    down(RUN - 3, 1, before_at[0])
                    row_and_up(RUN - 2, 1, at[1], last_load)
                    turn_mid(RUN - 2, 0)
                    down(RUN - 2, 2, before_at[1])
                    pe.wait_ge(rowlo_ready, base + RUN)
                    up(2, at[2])
                    turn_mid(RUN - 1, 1)
                    down(RUN - 1, 0, at[0])
                    turn_mid(RUN, 2)
                    down(RUN, 1, at[1])
                    down(RUN + 1, 2, at[2])
                    for reg in (*seen.values(), loads_seen):
                        pe.free_register(reg)


_INS = ['L0_attn_x', 'L0_attn_W1', 'L0_attn_b1', 'L0_attn_w2', 'L0_attn_b2', 'L0_attn_Wc', 'L0_attn_bc',
        'L0_ffn_W_in', 'L0_ffn_b_in', 'L0_ffn_W_gate', 'L0_ffn_b_gate', 'L0_ffn_W1', 'L0_ffn_b1',
        'L0_ffn_W2', 'L0_ffn_b2', 'L0_ffn_W_out', 'L0_ffn_b_out']


def kernel(**inputs):
    import numpy as np
    import concourse.bacc as bacc
    from concourse.bass_utils import run_bass_kernel_spmd

    nc = bacc.Bacc("TRN2", target_bir_lowering=False, num_devices=1)
    arrays, args = {}, []
    for name in _INS:
        a = np.ascontiguousarray(inputs[name])
        arrays[f"in_{name}"] = a
        args.append(nc.dram_tensor(f"in_{name}", a.shape, mybir.dt.from_np(a.dtype), kind="ExternalInput").ap())
    shape = arrays["in_L0_attn_x"].shape
    args.append(nc.dram_tensor("out_0", shape, mybir.dt.float32, kind="ExternalOutput").ap())
    build_program(nc, *args)
    r = run_bass_kernel_spmd(nc, [arrays], core_ids=[0])
    return r.results[0]["out_0"]
```
